# Optimizing a Trainium2 kernel written in Bass

```python
import numpy as np
import jax
import jax.numpy as jnp

def _softmax(x, axis=-1):
    return jax.nn.softmax(x, axis=axis)

def _gelu(x):
    return jax.nn.gelu(x, approximate=True)

def _silu(x):
    return jax.nn.silu(x)

def _sigmoid(x):
    return jax.nn.sigmoid(x)

def _layernorm(x, axis=-1, eps=1e-05):
    m = jnp.mean(x, axis=axis, keepdims=True)
    v = jnp.var(x, axis=axis, keepdims=True)
    return (x - m) / jnp.sqrt(v + eps)

def _scatter_add(tgt, idx, src, axis=0):
    return tgt.at[idx].add(src)

def _segment_sum(src, seg, n):
    return jax.ops.segment_sum(src, seg, n)
kernel_name = 'mk_prb_d1_jaxref_r8_287ab4'

def setup_inputs(seed: int=0):
    np.random.seed(seed)
    _w = jnp.asarray

    def _L0_attn_setup():
        import jax, jax.numpy as jnp
        import numpy as np
        DIM = 128
        NUM_HEADS = 16
        HEAD_DIM = DIM // NUM_HEADS
        PATCH_SIZE = 20
        SHIFT = 2
        B, N = (8, 512)

        def _patch_index(n, patch_size, shift):
            base = np.arange(0, patch_size * shift, shift, dtype=np.int64)[None, :]
            group = np.concatenate([base + i for i in range(shift)], axis=0)
            blocks = [group]
            idx = group
            while idx[-1, -1] < n:
                idx = idx + patch_size * shift
                blocks.append(idx)
            return np.concatenate(blocks, axis=0)
        PATCH_INDEX = _patch_index(N, PATCH_SIZE, SHIFT)
        PAD_SIZE = PATCH_SIZE * SHIFT - N % (PATCH_SIZE * SHIFT)
        key = jax.random.key(seed)
        k1, k2, k3 = jax.random.split(key, 3)
        x = jax.random.normal(k1, (B, N, DIM), dtype=jnp.float32)
        Wqkv = jax.random.normal(k2, (3 * DIM, DIM), dtype=jnp.float32) * 0.02
        Wout = jax.random.normal(k3, (DIM, DIM), dtype=jnp.float32) * 0.02
        bout = jnp.zeros((DIM,), dtype=jnp.float32)
        return {'x': x, 'Wqkv': Wqkv, 'Wout': Wout, 'bout': bout}
    _L0_attn_in = _L0_attn_setup()

    def _L0_ffn_setup():
        import jax, jax.numpy as jnp
        import numpy as np
        DIM = 128
        DEPTH = 2
        HEADS = 8
        DIM_HEAD = 64
        WINDOW = 64
        INNER = HEADS * DIM_HEAD
        HID = int(DIM * 4 * 2 / 3)
        B, N = (2, 1024)
        QK_SCALE = 8.0

        def shift_token(t):
            t1, t2 = jnp.split(t, 2, axis=-1)
            t2 = jnp.pad(t2, ((0, 0), (1, 0), (0, 0)))[:, :-1]
            return jnp.concatenate([t1, t2], axis=-1)

        def l2norm(t):
            return t / jnp.clip(jnp.linalg.norm(t, axis=-1, keepdims=True), 1e-12)

        def rotate_half(x):
            x1, x2 = jnp.split(x, 2, axis=-1)
            return jnp.concatenate([-x2, x1], axis=-1)

        def rotary_xpos(q, k):
            n = q.shape[-2]
            half_idx = jnp.arange(0, DIM_HEAD, 2, dtype=jnp.float32)
            inv_freq = 1.0 / 10000.0 ** (half_idx / DIM_HEAD)
            t = jnp.arange(n, dtype=jnp.float32)
            freqs = t[:, None] * inv_freq[None, :]
            freqs = jnp.concatenate([freqs, freqs], axis=-1)
            base = (half_idx + 0.4 * DIM_HEAD) / (1.4 * DIM_HEAD)
            power = (t - n // 2) / float(WINDOW // 2)
            scale = base[None, :] ** power[:, None]
            scale = jnp.concatenate([scale, scale], axis=-1)
            cos, sin = (jnp.cos(freqs), jnp.sin(freqs))
            q = q * cos * scale + rotate_half(q) * sin * scale
            k = k * cos / scale + rotate_half(k) * sin / scale
            return (q, k)

        def local_attention(q, k, v):
            b, h, n, d = q.shape
            w = n // WINDOW
            bq = q.reshape(b, h, w, WINDOW, d) * QK_SCALE
            bk = k.reshape(b, h, w, WINDOW, d)
            bv = v.reshape(b, h, w, WINDOW, d)

            def look_around(t):
                p = jnp.pad(t, ((0, 0), (0, 0), (1, 0), (0, 0), (0, 0)))
                return jnp.concatenate([p[:, :, :w], p[:, :, 1:]], axis=3)
            bk, bv = (look_around(bk), look_around(bv))
            bt = jnp.arange(n).reshape(w, WINDOW)
            btp = jnp.pad(bt, ((1, 0), (0, 0)), constant_values=-1)
            btk = jnp.concatenate([btp[:w], btp[1:]], axis=1)
            sim = jnp.einsum('bhwid,bhwjd->bhwij', bq, bk)
            i = bt[:, :, None]
            j = btk[:, None, :]
            mask = (i < j) | (i > j + WINDOW) | (j == -1)
            sim = jnp.where(mask, -jnp.finfo(sim.dtype).max, sim)
            attn = jax.nn.softmax(sim, axis=-1)
            out = jnp.einsum('bhwij,bhwjd->bhwid', attn, bv)
            return out.reshape(b, h, n, d)

        def _layer(x, wqkv, qs, ksc, wo, lg, lb, w1, b1, w2, b2):
            b, n, _ = x.shape
            h = shift_token(x)
            qkv = h @ wqkv
            q, k, v = jnp.split(qkv, 3, axis=-1)
            to_heads = lambda t: t.reshape(b, n, HEADS, DIM_HEAD).transpose(0, 2, 1, 3)
            q, k, v = (to_heads(q), to_heads(k), to_heads(v))
            q = l2norm(q) * qs
            k = l2norm(k) * ksc
            q, k = rotary_xpos(q, k)
            o = local_attention(q, k, v)
            o = o.transpose(0, 2, 1, 3).reshape(b, n, INNER)
            x = x + o @ wo
            h = shift_token(x)
            mu = h.mean(-1, keepdims=True)
            var = h.var(-1, keepdims=True)
            h = (h - mu) / jnp.sqrt(var + 1e-05) * lg + lb
            h = h @ w1 + b1
            a, g = jnp.split(h, 2, axis=-1)
            h = a * jax.nn.gelu(g, approximate=False)
            x = x + h @ w2 + b2
            return x
        key = jax.random.key(seed)
        ks = jax.random.split(key, 6)
        return {'x': jax.random.normal(ks[0], (B, N, DIM), jnp.float32), 'wqkv': jax.random.normal(ks[1], (DEPTH, DIM, 3 * INNER), jnp.float32) * 0.02, 'q_scale': jnp.ones((DEPTH, DIM_HEAD), jnp.float32), 'k_scale': jnp.ones((DEPTH, DIM_HEAD), jnp.float32), 'wo': jax.random.normal(ks[2], (DEPTH, INNER, DIM), jnp.float32) * 0.02, 'ln_g': jnp.ones((DEPTH, DIM), jnp.float32), 'ln_b': jnp.zeros((DEPTH, DIM), jnp.float32), 'w1': jax.random.normal(ks[3], (DEPTH, DIM, 2 * HID), jnp.float32) * 0.02, 'b1': jnp.zeros((DEPTH, 2 * HID), jnp.float32), 'w2': jax.random.normal(ks[4], (DEPTH, HID, DIM), jnp.float32) * 0.02, 'b2': jnp.zeros((DEPTH, DIM), jnp.float32)}
    _L0_ffn_in = _L0_ffn_setup()
    _d = {'L0_attn_x': _L0_attn_in['x'], 'L0_attn_Wqkv': _L0_attn_in['Wqkv'], 'L0_attn_Wout': _L0_attn_in['Wout'], 'L0_attn_bout': _L0_attn_in['bout'], 'L0_ffn_wqkv': _L0_ffn_in['wqkv'], 'L0_ffn_q_scale': _L0_ffn_in['q_scale'], 'L0_ffn_k_scale': _L0_ffn_in['k_scale'], 'L0_ffn_wo': _L0_ffn_in['wo'], 'L0_ffn_ln_g': _L0_ffn_in['ln_g'], 'L0_ffn_ln_b': _L0_ffn_in['ln_b'], 'L0_ffn_w1': _L0_ffn_in['w1'], 'L0_ffn_b1': _L0_ffn_in['b1'], 'L0_ffn_w2': _L0_ffn_in['w2'], 'L0_ffn_b2': _L0_ffn_in['b2']}
    _x0 = _d['L0_attn_x']
    _d['L0_attn_x'] = jax.random.normal(jax.random.fold_in(jax.random.key(seed), 1), (1, 2048, 128), dtype=_x0.dtype)
    del _x0
    return _d

def reference(L0_attn_x, L0_attn_Wqkv, L0_attn_Wout, L0_attn_bout, L0_ffn_wqkv, L0_ffn_q_scale, L0_ffn_k_scale, L0_ffn_wo, L0_ffn_ln_g, L0_ffn_ln_b, L0_ffn_w1, L0_ffn_b1, L0_ffn_w2, L0_ffn_b2):

    def _L0_attn_ref(x, Wqkv, Wout, bout):
        import jax, jax.numpy as jnp
        import numpy as np
        DIM = 128
        NUM_HEADS = 16
        HEAD_DIM = DIM // NUM_HEADS
        PATCH_SIZE = 20
        SHIFT = 2
        B, N = (8, 512)

        def _patch_index(n, patch_size, shift):
            base = np.arange(0, patch_size * shift, shift, dtype=np.int64)[None, :]
            group = np.concatenate([base + i for i in range(shift)], axis=0)
            blocks = [group]
            idx = group
            while idx[-1, -1] < n:
                idx = idx + patch_size * shift
                blocks.append(idx)
            return np.concatenate(blocks, axis=0)
        PATCH_INDEX = _patch_index(N, PATCH_SIZE, SHIFT)
        PAD_SIZE = PATCH_SIZE * SHIFT - N % (PATCH_SIZE * SHIFT)
        Bq, Nq, C = x.shape
        scale = HEAD_DIM ** (-0.5)
        pidx = jnp.asarray(PATCH_INDEX)
        x_pad = jnp.concatenate([x, jnp.zeros((Bq, PAD_SIZE, C), dtype=x.dtype)], axis=1)
        xp = x_pad[:, pidx, :]
        qkv = jnp.einsum('brsc,dc->brsd', xp, Wqkv)
        Rr, Sp = pidx.shape
        qkv = qkv.reshape(Bq, Rr, Sp, 3, NUM_HEADS, HEAD_DIM)
        q = qkv[..., 0, :, :].transpose(0, 1, 3, 2, 4)
        k = qkv[..., 1, :, :].transpose(0, 1, 3, 2, 4)
        v = qkv[..., 2, :, :].transpose(0, 1, 3, 2, 4)
        dots = jnp.einsum('brhsd,brhtd->brhst', q, k) * scale
        attn = jax.nn.softmax(dots, axis=-1)
        out = jnp.einsum('brhst,brhtd->brhsd', attn, v)
        out = out.transpose(0, 1, 3, 2, 4).reshape(Bq, Rr, Sp, C)
        x_pad = x_pad.at[:, pidx.reshape(-1), :].set(out.reshape(Bq, -1, C))
        return x_pad[:, :Nq, :] @ Wout.T + bout

    def _L0_ffn_ref(x, wqkv, q_scale, k_scale, wo, ln_g, ln_b, w1, b1, w2, b2):
        import jax, jax.numpy as jnp
        import numpy as np
        DIM = 128
        DEPTH = 2
        HEADS = 8
        DIM_HEAD = 64
        WINDOW = 64
        INNER = HEADS * DIM_HEAD
        HID = int(DIM * 4 * 2 / 3)
        B, N = (2, 1024)
        QK_SCALE = 8.0

        def shift_token(t):
            t1, t2 = jnp.split(t, 2, axis=-1)
            t2 = jnp.pad(t2, ((0, 0), (1, 0), (0, 0)))[:, :-1]
            return jnp.concatenate([t1, t2], axis=-1)

        def l2norm(t):
            return t / jnp.clip(jnp.linalg.norm(t, axis=-1, keepdims=True), 1e-12)

        def rotate_half(x):
            x1, x2 = jnp.split(x, 2, axis=-1)
            return jnp.concatenate([-x2, x1], axis=-1)

        def rotary_xpos(q, k):
            n = q.shape[-2]
            half_idx = jnp.arange(0, DIM_HEAD, 2, dtype=jnp.float32)
            inv_freq = 1.0 / 10000.0 ** (half_idx / DIM_HEAD)
            t = jnp.arange(n, dtype=jnp.float32)
            freqs = t[:, None] * inv_freq[None, :]
            freqs = jnp.concatenate([freqs, freqs], axis=-1)
            base = (half_idx + 0.4 * DIM_HEAD) / (1.4 * DIM_HEAD)
            power = (t - n // 2) / float(WINDOW // 2)
            scale = base[None, :] ** power[:, None]
            scale = jnp.concatenate([scale, scale], axis=-1)
            cos, sin = (jnp.cos(freqs), jnp.sin(freqs))
            q = q * cos * scale + rotate_half(q) * sin * scale
            k = k * cos / scale + rotate_half(k) * sin / scale
            return (q, k)

        def local_attention(q, k, v):
            b, h, n, d = q.shape
            w = n // WINDOW
            bq = q.reshape(b, h, w, WINDOW, d) * QK_SCALE
            bk = k.reshape(b, h, w, WINDOW, d)
            bv = v.reshape(b, h, w, WINDOW, d)

            def look_around(t):
                p = jnp.pad(t, ((0, 0), (0, 0), (1, 0), (0, 0), (0, 0)))
                return jnp.concatenate([p[:, :, :w], p[:, :, 1:]], axis=3)
            bk, bv = (look_around(bk), look_around(bv))
            bt = jnp.arange(n).reshape(w, WINDOW)
            btp = jnp.pad(bt, ((1, 0), (0, 0)), constant_values=-1)
            btk = jnp.concatenate([btp[:w], btp[1:]], axis=1)
            sim = jnp.einsum('bhwid,bhwjd->bhwij', bq, bk)
            i = bt[:, :, None]
            j = btk[:, None, :]
            mask = (i < j) | (i > j + WINDOW) | (j == -1)
            sim = jnp.where(mask, -jnp.finfo(sim.dtype).max, sim)
            attn = jax.nn.softmax(sim, axis=-1)
            out = jnp.einsum('bhwij,bhwjd->bhwid', attn, bv)
            return out.reshape(b, h, n, d)

        def _layer(x, wqkv, qs, ksc, wo, lg, lb, w1, b1, w2, b2):
            b, n, _ = x.shape
            h = shift_token(x)
            qkv = h @ wqkv
            q, k, v = jnp.split(qkv, 3, axis=-1)
            to_heads = lambda t: t.reshape(b, n, HEADS, DIM_HEAD).transpose(0, 2, 1, 3)
            q, k, v = (to_heads(q), to_heads(k), to_heads(v))
            q = l2norm(q) * qs
            k = l2norm(k) * ksc
            q, k = rotary_xpos(q, k)
            o = local_attention(q, k, v)
            o = o.transpose(0, 2, 1, 3).reshape(b, n, INNER)
            x = x + o @ wo
            h = shift_token(x)
            mu = h.mean(-1, keepdims=True)
            var = h.var(-1, keepdims=True)
            h = (h - mu) / jnp.sqrt(var + 1e-05) * lg + lb
            h = h @ w1 + b1
            a, g = jnp.split(h, 2, axis=-1)
            h = a * jax.nn.gelu(g, approximate=False)
            x = x + h @ w2 + b2
            return x
        for l in range(DEPTH):
            x = _layer(x, wqkv[l], q_scale[l], k_scale[l], wo[l], ln_g[l], ln_b[l], w1[l], b1[l], w2[l], b2[l])
        return x
    x = L0_attn_x
    xn = _layernorm(x, axis=-1)
    x = x + _L0_attn_ref(xn, L0_attn_Wqkv, L0_attn_Wout, L0_attn_bout) + _L0_ffn_ref(xn, L0_ffn_wqkv, L0_ffn_q_scale, L0_ffn_k_scale, L0_ffn_wo, L0_ffn_ln_g, L0_ffn_ln_b, L0_ffn_w1, L0_ffn_b1, L0_ffn_w2, L0_ffn_b2)
    return x

_drawn_inputs = setup_inputs


def setup_inputs(seed=0):
    import zlib

    import numpy as np

    out = dict(_drawn_inputs(seed))
    spreads = {'L0_attn_bout': (0.0, 0.8),
     'L0_ffn_q_scale': (1.0, 0.6),
     'L0_ffn_k_scale': (1.0, 0.6),
     'L0_ffn_ln_g': (1.0, 0.6),
     'L0_ffn_ln_b': (0.0, 0.8),
     'L0_ffn_b1': (0.0, 0.8),
     'L0_ffn_b2': (0.0, 0.408)}
    factors = {'L0_attn_Wqkv': 45.114,
     'L0_ffn_wqkv': 4.136,
     'L0_ffn_wo': 4.116,
     'L0_ffn_w1': 6.192,
     'L0_ffn_w2': 6.096,
     'L0_attn_Wout': 3.359}
    for name, (base, spread) in spreads.items():
        noise = np.random.default_rng([zlib.crc32(name.encode()), seed]).standard_normal(out[name].shape)
        drawn = base * np.exp(spread * noise) if base else spread * noise
        out[name] = jnp.asarray(drawn.astype(out[name].dtype))
    for name, factor in factors.items():
        out[name] = (out[name] * factor).astype(out[name].dtype)
    return out
```

```python
from contextlib import ExitStack

import numpy as np

import concourse.bass as bass
import concourse.mybir as mybir
from concourse.alu_op_type import AluOpType as ALU

F32 = mybir.dt.float32
BF16 = mybir.dt.bfloat16
ACT = mybir.ActivationFunctionType
AX = mybir.AxisListType

P = 128
N = 2048
DIM = 128
TILES = N // P
LAYERS = 2
HEADS, DH = 8, 64
HALF = DH // 2
INNER = HEADS * DH
WINDOW = 64
CHUNKS = INNER // P
QK_SCALE = 8.0
HID = int(DIM * 4 * 2 / 3)
HID_PARTS = [(0, 128), (128, 128), (256, HID - 256)]
LN_EPS = 1e-5
WIDE = 512
SPANS = N // WIDE
MASKED = -1e30

PATCH, SHIFT = 20, 2
BLOCK = PATCH * SHIFT
PATCH_BLOCKS = 13
PATCHED = PATCH_BLOCKS * BLOCK
A_HEADS, A_DH = 16, 8
A_SCALE = A_DH ** -0.5
A_STEP = 2 * BLOCK
A_STEPS = -(-PATCHED // A_STEP)
A_WIN = 112
QUADS = 4

LN_SHIFT = 2.0 ** 16
LN_UNSHIFT = float(np.log(2.0 ** 8))
NORM_FLOOR_SQ = 1e-24


def constants():
    half_idx = np.arange(0, DH, 2, dtype=np.float32)
    inv_freq = (1.0 / 10000.0 ** (half_idx / DH)).astype(np.float32)
    t = np.arange(N, dtype=np.float32)
    freqs = (t[:, None] * inv_freq[None, :]).astype(np.float32).astype(np.float64)
    base = (half_idx.astype(np.float64) + 0.4 * DH) / (1.4 * DH)
    scale = base[None, :] ** ((t.astype(np.float64)[:, None] - N // 2) / (WINDOW // 2))
    cos, sin = np.cos(freqs), np.sin(freqs)

    def table(parts):
        full = np.stack([np.concatenate(x, 1) for x in parts], 1).astype(np.float32)
        return np.ascontiguousarray(full.reshape(TILES, P, 2, DH).transpose(1, 0, 2, 3))

    qs, ks = scale * QK_SCALE, 1.0 / scale
    cos_t = table([(cos * qs, cos * qs), (cos * ks, cos * ks)])
    sin_t = table([(sin * qs, -sin * qs), (sin * ks, -sin * ks)])

    ident = np.eye(P, dtype=np.float32)
    i = np.arange(P)[:, None] % WINDOW
    j = np.arange(2 * WINDOW)[None, :]
    usual = np.where((j >= i) & (j <= i + WINDOW), 0.0, MASKED)
    first = np.where((j >= WINDOW) & (j <= i + WINDOW), 0.0, MASKED)
    mask = np.stack([np.tile(usual, (1, 4)), np.concatenate([first, usual] * 2, 1)], 1)
    center = ident - 1.0 / P
    mean = np.full((P, P), 1.0 / P, np.float32)
    head_of = (np.arange(P)[:, None] % 32) // A_DH == np.arange(4)[None, :]
    key_head = np.arange(4 * PATCH) // PATCH
    value_head = (np.arange(P) % 32) // A_DH
    value_mask = np.zeros((P, P), np.float32)
    value_mask[:4 * PATCH] = key_head[:, None] == value_head[None, :]
    small = np.concatenate([ident, center, mean, value_mask, head_of], 1).astype(np.float32)
    masks = np.concatenate([ident, mask.reshape(P, -1)], 1).astype(np.float32)
    return {"cos_t": cos_t, "sin_t": sin_t, "small": small, "masks": masks}


def pack_vectors(ffn_b1, ffn_ln_g, ffn_ln_b, ffn_b2, attn_bout):
    b1 = np.zeros((LAYERS, 2, 3 * P), np.float32)
    b1[:, :, :HID] = np.reshape(ffn_b1, (LAYERS, 2, HID))
    rows = [b1.reshape(12, P), ffn_ln_g, ffn_ln_b, ffn_b2, np.reshape(attn_bout, (1, P))]
    return np.concatenate([np.asarray(r) for r in rows], 0).T


def after(eng, sem, count):
    if not isinstance(count, int) or count > 0:
        eng.wait_ge(sem, count)


def over_tiles(eng, layer, start, step):
    n0 = layer * TILES
    start(n0, 0, 0)
    step(n0, 0, 0, True, False)
    step(n0 + 1, 1, 1, False, False)
    with eng.Fori(1, TILES // 2 - 1) as i:
        step(i * 2 + n0, i * 2, 0, False, False)
        step(i * 2 + (n0 + 1), i * 2 + 1, 1, False, False)
    step(n0 + TILES - 2, TILES - 2, 0, False, False)
    step(n0 + TILES - 1, TILES - 1, 1, False, True)


def cols(start, size):
    return slice(start, start + size) if isinstance(start, int) else bass.ds(start, size)


def build(nc, x, a_wqkv_t, a_wout_t, wqkv, q_scale, k_scale, wo, w1, w2, vectors_d,
          cos_d, sin_d, small_d, masks_d, out):
    ctx = ExitStack()
    with ctx:
        def sb(name, shape, dt=F32):
            return ctx.enter_context(nc.sbuf_tensor(name, shape, dt))

        def sem(name):
            return ctx.enter_context(nc.semaphore(name))

        small = sb("small", [P, 4 * P + 4])
        ident, center_w, mean_w = small[:, 0:P], small[:, P:2 * P], small[:, 2 * P:3 * P]
        value_mask, head_mask = small[:, 3 * P:4 * P], small[:, 4 * P:4 * P + 4]
        masks = sb("masks", [P, P + 2 * WIDE], BF16)
        ident_bf, usual_mask, first_mask = masks[:, 0:P], masks[:, P:P + WIDE], masks[:, P + WIDE:]
        cos_raw = sb("cos_raw", [P, TILES, 2, DH])
        sin_raw = sb("sin_raw", [P, TILES, 2, DH])
        cos_w = sb("cos_w", [P, TILES, 2, DH])
        sin_w = sb("sin_w", [P, TILES, 2, DH])
        qk_scale = sb("qk_scale", [P, LAYERS, 2, DH])
        a_wqkv_s = sb("a_wqkv_s", [P, 3 * DIM])
        a_wout_s = sb("a_wout_s", [P, DIM])
        wqkv_s = sb("wqkv_s", [P, LAYERS, 3 * INNER])
        wo_s = sb("wo_s", [P, LAYERS, CHUNKS, DIM])
        w1_s = sb("w1_s", [P, LAYERS, 2 * HID])
        w2_s = sb("w2_s", [P, LAYERS, 3, DIM])
        vectors = sb("vectors", [P, 19])
        b1_s = vectors[:, 0:12].rearrange("p (l a c) -> p l a c", l=LAYERS, a=2)
        vec_s = vectors[:, 12:19]
        b2_out = sb("b2_out", [P, 1])
        eps_s = sb("eps_s", [P, 2])

        x_raw = sb("x_raw", [P, TILES, DIM])
        xn_tok = sb("xn_tok", [P, TILES, DIM])
        stats = sb("stats", [P, TILES, 6])
        mv = sb("mv", [P, TILES, 2])
        ln0 = sb("ln0", [P, TILES])
        rstd0 = sb("rstd0", [P, TILES])
        xin = sb("xin", [P, 1 + N])
        x1 = sb("x1", [P, N])
        masks_f = x1[:, 0:P + 2 * WIDE]
        x1_shift = sb("x1_shift", [P, 1 + N])
        x_patch = sb("x_patch", [P, N])
        hn = xn_tok[:].rearrange("p t d -> p (t d)")

        stage = [sb(f"stage{i}", [P, P]) for i in range(2)]
        sq = sb("sq", [P, 2 * INNER])
        ss = sb("ss", [P, 2 * HEADS])
        ssc = sb("ssc", [P, 2 * HEADS])
        lnss = sb("lnss", [P, 2 * HEADS])
        rnorm = sb("rnorm", [P, 2 * HEADS])
        qkn = sb("qkn", [P, 2 * INNER])
        rot1 = sb("rot1", [P, 2 * INNER])
        rot2 = sb("rot2", [P, 2 * INNER])
        q_diag = [sb(f"q_diag{i}", [P, CHUNKS, 2, P]) for i in range(2)]
        k_t = [sb(f"k_t{i}", [P, CHUNKS, WINDOW + P]) for i in range(2)]
        v_tok = [sb(f"v_tok{i}", [P, INNER]) for i in range(2)]
        v_off = [sb(f"v_off{i}", [P, INNER]) for i in range(2)]
        neg_max = sb("neg_max", [P, 8])
        row_sum = sb("row_sum", [P, 8])
        row_inv = sb("row_inv", [P, 8])
        probs = sb("probs", [P, 8, P])
        probs_n = sb("probs_n", [P, 8, P])
        probs_t = sb("probs_t", [P, 8, P])
        o_t = sb("o_t", [P, INNER])

        ln_sq = [sb(f"ln_sq{i}", [P, WIDE]) for i in range(2)]
        ln_log = [sb(f"ln_log{i}", [P, WIDE]) for i in range(2)]
        ln_rstd = [sb(f"ln_rstd{i}", [P, WIDE]) for i in range(2)]
        gelu_s = [sb(f"gelu{i}", [P, WIDE]) for i in range(2)]
        hh = sb("hh", [P, 3, WIDE])
        sum_t = sb("sum_t", [P, WIDE])
        out_s = sb("out_s", [P, WIDE])

        a_x = sb("a_x", [P, A_WIN])
        a_rep = sb("a_rep", [P, 4, 4, PATCH])
        a_q = sb("a_q", [P, A_WIN])
        a_k = sb("a_k", [P, 4, A_WIN])
        a_v = sb("a_v", [4 * PATCH, 4, DIM])
        a_max = sb("a_max", [P, A_HEADS])
        a_dif = sb("a_dif", [P, A_HEADS, PATCH])
        a_p = sb("a_p", [P, A_HEADS, PATCH])
        a_sum = sb("a_sum", [P, A_HEADS])
        a_inv = sb("a_inv", [P, A_HEADS])
        a_pn = sb("a_pn", [P, A_HEADS, PATCH])
        a_pt = sb("a_pt", [4 * PATCH, WIDE])
        a_o = sb("a_o", [P, DIM])

        ps = ctx.enter_context(nc.psum_tensor("ps", [P, 8 * WIDE], F32))

        def bank(b, n=1):
            return ps[:, b * WIDE:(b + n) * WIDE]

        qk_ps = bank(0, 2)
        v_ps = bank(2)
        s_ps = [bank(3), bank(4)]
        ot_ps = bank(5)
        y_ps = bank(6)
        cen_ps = [bank(0), bank(1)]
        var_ps = [bank(2), bank(3)]
        gate_ps = [bank(0), bank(1)]
        lin_ps = [bank(2), bank(3)]
        ffn_ps = bank(4)
        tr_ps = bank(5)
        a_s = bank(0, 4).rearrange("p (g c) -> p g c", g=4)[:, :, 0:4 * PATCH]
        a_q_ps = bank(4)[:, 0:A_WIN]
        a_k_ps = bank(5)[:, 0:A_WIN]
        a_vr = bank(6)
        a_tp = bank(4)
        a_op = bank(7)
        t0_ps = [bank(0), bank(1)]

        x_in = sem("x_in")
        const_in = sem("const_in")
        aw_in = sem("aw_in")
        tab_in = sem("tab_in")
        w_in = sem("w_in")
        fw_in = sem("fw_in")
        zeroed = sem("zeroed")
        stat_done = sem("stat_done")
        mv_done = sem("mv_done")
        ln0_done = sem("ln0_done")
        rstd0_done = sem("rstd0_done")
        xn_done = sem("xn_done")
        xn_tr = sem("xn_tr")
        xin0_done = sem("xin0_done")
        a_staged = sem("a_staged")
        a_qk_done = sem("a_qk_done")
        a_vr_done = sem("a_vr_done")
        a_q_done = sem("a_q_done")
        a_k_done = sem("a_k_done")
        a_v_done = sem("a_v_done")
        a_s_done = sem("a_s_done")
        a_max_done = sem("a_max_done")
        a_dif_done = sem("a_dif_done")
        a_p_done = sem("a_p_done")
        a_sum_done = sem("a_sum_done")
        a_inv_done = sem("a_inv_done")
        a_pn_done = sem("a_pn_done")
        a_tp_done = sem("a_tp_done")
        a_pt_done = sem("a_pt_done")
        a_op_done = sem("a_op_done")
        a_o_done = sem("a_o_done")
        a_ot_done = sem("a_ot_done")
        a_out_done = sem("a_out_done")
        patch_done = sem("patch_done")
        tables_done = sem("tables_done")
        masks_done = sem("masks_done")
        staged = sem("staged")
        qk_ready = sem("qk_ready")
        v_ready = sem("v_ready")
        sq_done = sem("sq_done")
        ss_done = sem("ss_done")
        lnss_done = sem("lnss_done")
        rnorm_done = sem("rnorm_done")
        qkn_done = sem("qkn_done")
        rot_done = sem("rot_done")
        qkt_ready = sem("qkt_ready")
        qkt_evac = sem("qkt_evac")
        v_evac = sem("v_evac")
        v_off_in = sem("v_off_in")
        s_ready = sem("s_ready")
        max_done = sem("max_done")
        probs_done = sem("probs_done")
        inv_done = sem("inv_done")
        probs_n_done = sem("probs_n_done")
        pt_ready = sem("pt_ready")
        pt_evac = sem("pt_evac")
        ot_ready = sem("ot_ready")
        ot_evac = sem("ot_evac")
        y_ready = sem("y_ready")
        x1_done = sem("x1_done")
        x1_shifted = sem("x1_shifted")
        cen_ready = sem("cen_ready")
        ln_sq_done = sem("ln_sq_done")
        var_ready = sem("var_ready")
        ln_log_done = sem("ln_log_done")
        ln_rstd_done = sem("ln_rstd_done")
        hn_scaled = sem("hn_scaled")
        hn_done = sem("hn_done")
        gate_ready = sem("gate_ready")
        lin_ready = sem("lin_ready")
        gelu_done = sem("gelu_done")
        hh_done = sem("hh_done")
        ffn_ready = sem("ffn_ready")
        x2_done = sem("x2_done")
        tr_ready = sem("tr_ready")
        out_done = sem("out_done")
        stored = sem("stored")

        block = ctx.enter_context(nc.Block())

        @block.sync
        def _(sp):
            sp.dma_start(x_raw[:], x.rearrange("a (t p) d -> p (a t) d", p=P)).then_inc(x_in, 16)
            sp.dma_start(small[:], small_d).then_inc(const_in, 16)
            sp.dma_start(masks_f, masks_d).then_inc(const_in, 16)
            sp.dma_start(a_wqkv_s[:], a_wqkv_t).then_inc(aw_in, 16)
            sp.dma_start(cos_raw[:], cos_d).then_inc(tab_in, 16)
            sp.dma_start(sin_raw[:], sin_d).then_inc(tab_in, 16)
            for part, scale in enumerate((q_scale, k_scale)):
                sp.dma_start(qk_scale[:, :, part, :], scale.partition_broadcast(P)).then_inc(tab_in, 16)
            sp.dma_start(wqkv_s[:], wqkv.rearrange("l p n -> p l n")).then_inc(w_in, 16)
            sp.dma_start(wo_s[:], wo.rearrange("l (c p) n -> p l c n", p=P)).then_inc(w_in, 16)
            sp.dma_start(w1_s[:], w1.rearrange("l p n -> p l n")).then_inc(fw_in, 16)
            sp.dma_start(a_wout_s[:], a_wout_t).then_inc(fw_in, 16)
            for c, (at, size) in enumerate(HID_PARTS):
                sp.dma_start(w2_s[0:size, :, c, :],
                             w2[:, at:at + size, :].rearrange("l p n -> p l n")).then_inc(fw_in, 16)
            sp.dma_start(vectors[:], vectors_d).then_inc(fw_in, 16)

            def shift_values(n, parity):
                after(sp, v_evac, n + 1)
                sp.dma_start(v_off[parity][0:WINDOW, :], v_tok[1 - parity][WINDOW:P, :]).then_inc(v_off_in, 16)
                sp.dma_start(v_off[parity][WINDOW:P, :], v_tok[parity][0:WINDOW, :]).then_inc(v_off_in, 16)

            def start(n, t, parity):
                shift_values(n, parity)

            def step(n, t, parity, first, last):
                if not last:
                    shift_values(n + 1, 1 - parity)

            sp.wait_ge(zeroed, 5)
            for layer in range(LAYERS):
                over_tiles(sp, layer, start, step)
            for j in range(SPANS):
                sp.wait_ge(out_done, j + 1)
                sp.dma_start(out[0, cols(j * WIDE, WIDE), :].rearrange("(q p) d -> p q d", p=P),
                             out_s[:].rearrange("p (q d) -> p q d", q=4)).then_inc(stored, 16)
            sp.wait_ge(stored, 16 * SPANS)

        @block.gpsimd
        def _(pool):
            pool.memset(xin[:, 0:1], 0.0).then_inc(zeroed, 1)
            pool.memset(x1_shift[:, 0:1], 0.0).then_inc(zeroed, 1)
            pool.memset(v_tok[1][:], 0.0).then_inc(zeroed, 1)
            pool.memset(k_t[0][:], 0.0).then_inc(zeroed, 1)
            pool.memset(eps_s[:, 0:1], LN_EPS).then_inc(zeroed, 1)
            pool.memset(eps_s[:, 1:2], LN_UNSHIFT).then_inc(zeroed, 1)
            for parity in range(2):
                pool.memset(q_diag[parity][:], 0.0).then_inc(zeroed, 1)

            def make_stage(layer, n, t, parity, own_done):
                after(pool, probs_n_done, own_done)
                after(pool, v_ready, n - 1)
                pool.tensor_copy(stage[parity][0:64, :], xin[0:64, cols(t * P + 1, P)]).then_inc(staged, 1)
                pool.tensor_copy(stage[parity][64:P, :], xin[64:P, cols(t * P, P)]).then_inc(staged, 1)

            def normalize(n, g, own_done):
                after(pool, staged, own_done)
                after(pool, x1_shifted, 2 * n)
                after(pool, inv_done, 2 * n + (g + 1))
                after(pool, pt_ready, 2 * n + (g - 1))
                pool.tensor_tensor(probs_n[:, 4 * g:4 * g + 4, :], probs[:, 4 * g:4 * g + 4, :],
                                   row_inv[:, 4 * g:4 * g + 4].unsqueeze(2).broadcast_to([P, 4, P]),
                                   ALU.mult).then_inc(probs_n_done, 1)

            def shift_x1(n, t):
                after(pool, x1_done, n + 1)
                pool.tensor_copy(x1_shift[0:64, cols(t * P, P)], x1[0:64, cols(t * P, P)]).then_inc(x1_shifted, 1)
                pool.tensor_copy(x1_shift[64:P, cols(t * P + 1, P)], x1[64:P, cols(t * P, P)]).then_inc(x1_shifted, 1)

            for layer in range(LAYERS):
                if layer == 0:
                    pool.wait_ge(xin0_done, SPANS)
                else:
                    pool.wait_ge(x2_done, SPANS)

                def start(n, t, parity):
                    make_stage(layer, n, t, parity, 2 * n)
                    make_stage(layer, n + 1, t + 1, 1 - parity, 2 * n)

                def step(n, t, parity, first, last):
                    for g in range(2):
                        normalize(n, g, 2 * n + (2 if last else 4))
                    if not (isinstance(t, int) and t + 2 >= TILES):
                        make_stage(layer, n + 2, t + 2, parity, 2 * n + 2)
                    else:
                        pool.wait_ge(probs_n_done, 2 * n + 2)
                    shift_x1(n, t)

                over_tiles(pool, layer, start, step)

        @block.tensor
        def _(pe):
            pe.wait_ge(const_in, 32)
            for g in range(SPANS):
                pe.wait_ge(xn_done, 4 * g + 4)
                if g >= 2:
                    pe.wait_ge(xin0_done, g - 1)
                for q in range(4):
                    mm = pe.transpose(t0_ps[g % 2][:, q * P:(q + 1) * P], xn_tok[:, 4 * g + q, :], ident)
                mm.then_inc(xn_tr, 1)

            pe.wait_ge(aw_in, 16)
            pe.wait_ge(xin0_done, SPANS)
            with pe.Fori(0, A_STEPS) as it:
                after(pe, a_staged, 3 * it + 3)
                pe.matmul(a_q_ps, a_wqkv_s[:, 0:DIM], a_x[:], start=True, stop=True)
                pe.matmul(a_k_ps, a_wqkv_s[:, DIM:2 * DIM], a_x[:],
                          start=True, stop=True).then_inc(a_qk_done, 1)
                after(pe, a_q_done, it + 1)
                after(pe, a_k_done, it + 1)
                for j in range(4):
                    mm = pe.matmul(a_vr[0:4 * PATCH, j * DIM:(j + 1) * DIM],
                                   a_rep[:, j, :, :].rearrange("p r i -> p (r i)"),
                                   a_wqkv_s[:, 2 * DIM:3 * DIM], start=True, stop=True)
                mm.then_inc(a_vr_done, 1)
                for j in range(4):
                    at = BLOCK * (j // 2) + j % 2
                    for g in range(QUADS):
                        mm = pe.matmul(a_s[32 * j:32 * j + 32, g, :],
                                       a_q[32 * g:32 * g + 32, at:at + 63:SHIFT],
                                       a_k[32 * g:32 * g + 32, :, at:at + BLOCK - 1:SHIFT],
                                       start=True, stop=True)
                mm.then_inc(a_s_done, 1)
                after(pe, a_pn_done, it + 1)
                for g in range(QUADS):
                    mm = pe.transpose(a_tp[0:4 * PATCH, g * P:(g + 1) * P],
                                      a_pn[:, 4 * g:4 * g + 4, :].rearrange("p h k -> p (h k)"), ident)
                mm.then_inc(a_tp_done, 1)
                after(pe, a_pt_done, it + 1)
                after(pe, a_v_done, it + 1)
                for j in range(4):
                    for g in range(QUADS):
                        mm = pe.matmul(a_op[32 * j:32 * j + 32, 32 * g:32 * g + 32],
                                       a_pt[:, g * P + 32 * j:g * P + 32 * j + 32],
                                       a_v[:, j, 32 * g:32 * g + 32], start=True, stop=True)
                mm.then_inc(a_op_done, 1)
                after(pe, a_o_done, it + 1)
                pe.transpose(a_op[:, P:2 * P], a_o[:], ident).then_inc(a_ot_done, 1)
            pe.wait_ge(a_out_done, A_STEPS)

            pe.wait_ge(w_in, 32)
            pe.wait_ge(masks_done, 1)
            for layer in range(LAYERS):
                def project(n, parity):
                    after(pe, staged, 2 * n + 2)
                    after(pe, qkt_evac, 4 * n)
                    pe.matmul(qk_ps[:, 0:INNER], stage[parity][:], wqkv_s[:, layer, 0:INNER],
                              start=True, stop=True)
                    pe.matmul(qk_ps[:, INNER:], stage[parity][:], wqkv_s[:, layer, INNER:2 * INNER],
                              start=True, stop=True).then_inc(qk_ready, 1)
                    after(pe, v_evac, n)
                    pe.matmul(v_ps, stage[parity][:], wqkv_s[:, layer, 2 * INNER:],
                              start=True, stop=True).then_inc(v_ready, 1)

                def turn(n):
                    after(pe, rot_done, 3 * n + 3)
                    for part in range(2):
                        for c in range(CHUNKS):
                            at = part * INNER + c * P
                            pe.matmul(qk_ps[:, at:at + P], rot1[:, at:at + P], ident,
                                      start=True, stop=False, is_transpose=True)
                            mm = pe.matmul(qk_ps[:, at:at + P], rot2[:, at:at + P], ident,
                                           start=False, stop=True, is_transpose=True)
                        mm.then_inc(qkt_ready, 1)

                def scores(n, parity, g, first):
                    after(pe, qkt_evac, 4 * n + 4)
                    after(pe, pt_evac, 2 * n + (g - 1))
                    pe.matmul(s_ps[g], ident_bf, first_mask if first else usual_mask,
                              start=True, stop=False, skip_group_check=True)
                    for cw in range(4):
                        c, w = 2 * g + cw // 2, cw % 2
                        mm = pe.matmul(s_ps[g][:, cw * P:(cw + 1) * P], q_diag[parity][:, c, w, :],
                                       k_t[parity][:, c, w * WINDOW:w * WINDOW + P],
                                       start=False, stop=True, skip_group_check=True)
                    mm.then_inc(s_ready, 1)

                def turn_probs(n, g):
                    after(pe, probs_n_done, 2 * n + (g + 1))
                    for cw in range(4):
                        mm = pe.transpose(s_ps[g][:, cw * P:(cw + 1) * P], probs_n[:, 4 * g + cw, :], ident)
                    mm.then_inc(pt_ready, 1)

                def weigh_values(n, parity, g):
                    after(pe, pt_evac, 2 * n + (g + 1))
                    if g == 0:
                        after(pe, v_off_in, 32 * n + 32)
                        after(pe, ot_evac, n)
                    for cw in range(4):
                        c, w = 2 * g + cw // 2, cw % 2
                        v = (v_off if w == 0 else v_tok)[parity]
                        for h in range(2):
                            head = (2 * c + h) * DH
                            mm = pe.matmul(ot_ps[64 * h:64 * h + 64, c * P + w * WINDOW:c * P + (w + 1) * WINDOW],
                                           v[:, head:head + DH],
                                           probs_t[:, 4 * g + cw, h * WINDOW:(h + 1) * WINDOW],
                                           start=True, stop=True)
                    if g == 1:
                        mm.then_inc(ot_ready, 1)

                def project_out(n):
                    after(pe, ot_evac, n + 1)
                    after(pe, x1_done, n)
                    for c in range(CHUNKS):
                        mm = pe.matmul(y_ps[:, 0:P], wo_s[:, layer, c, :], o_t[:, c * P:(c + 1) * P],
                                       start=(c == 0), stop=(c == CHUNKS - 1))
                    mm.then_inc(y_ready, 1)

                def start(n, t, parity):
                    project(n, parity)
                    turn(n)

                def step(n, t, parity, first, last):
                    scores(n, parity, 0, first)
                    scores(n, parity, 1, first)
                    if not last:
                        project(n + 1, 1 - parity)
                    turn_probs(n, 0)
                    turn_probs(n, 1)
                    weigh_values(n, parity, 0)
                    if not last:
                        turn(n + 1)
                    weigh_values(n, parity, 1)
                    project_out(n)

                over_tiles(pe, layer, start, step)

                pe.wait_ge(x1_shifted, 2 * TILES * (layer + 1))

                def centered(j):
                    jj = SPANS * layer + j
                    after(pe, hn_scaled, jj - 1)
                    pe.matmul(cen_ps[j % 2], center_w, x1_shift[:, j * WIDE:(j + 1) * WIDE],
                              start=True, stop=True).then_inc(cen_ready, 1)

                centered(0)
                for j in range(SPANS):
                    jj = SPANS * layer + j
                    if j + 1 < SPANS:
                        centered(j + 1)
                    after(pe, ln_sq_done, jj + 1)
                    after(pe, ln_log_done, jj - 1)
                    pe.matmul(var_ps[j % 2], mean_w, ln_sq[j % 2][:], start=True, stop=True).then_inc(var_ready, 1)

                if layer == 0:
                    pe.wait_ge(fw_in, 16 * 6)
                pe.wait_ge(hn_done, SPANS * (layer + 1))
                if layer == LAYERS - 1:
                    pe.wait_ge(patch_done, 1)
                with pe.Fori(0, SPANS) as j:
                    jj = j + SPANS * layer
                    for c, (at, size) in enumerate(HID_PARTS):
                        after(pe, hh_done, 3 * jj if c < 2 else 3 * jj + 1)
                        pe.matmul(gate_ps[c % 2][0:size, :], w1_s[:, layer, HID + at:HID + at + size],
                                  hn[:, cols(j * WIDE, WIDE)], start=True, stop=True).then_inc(gate_ready, 1)
                        pe.matmul(lin_ps[c % 2][0:size, :], w1_s[:, layer, at:at + size],
                                  hn[:, cols(j * WIDE, WIDE)], start=True, stop=True).then_inc(lin_ready, 1)
                    after(pe, x2_done, jj)
                    if layer == LAYERS - 1:
                        pe.matmul(ffn_ps, a_wout_s[:], x_patch[:, cols(j * WIDE, WIDE)], start=True, stop=False)
                    for c, (at, size) in enumerate(HID_PARTS):
                        after(pe, hh_done, 3 * jj + (c + 1))
                        mm = pe.matmul(ffn_ps, w2_s[0:size, layer, c, :], hh[0:size, c, :],
                                       start=(c == 0 and layer < LAYERS - 1), stop=(c == 2))
                    mm.then_inc(ffn_ready, 1)
                    if layer == LAYERS - 1:
                        after(pe, x2_done, jj + 1)
                        after(pe, out_done, j)
                        for q in range(4):
                            mm = pe.transpose(tr_ps[:, q * P:(q + 1) * P], sum_t[:, q * P:(q + 1) * P], ident)
                        mm.then_inc(tr_ready, 1)

        @block.scalar
        def _(act):
            act.preload_act_table_set("natural_log_exp_and_others")
            act.wait_ge(zeroed, 8)
            act.wait_ge(mv_done, TILES)
            act.activation(ln0[:], mv[:, :, 1], ACT.Ln, bias=eps_s[:, 0:1]).then_inc(ln0_done, 1)
            act.wait_ge(ln0_done, 1)
            act.activation(rstd0[:], ln0[:], ACT.Exp, scale=-0.5).then_inc(rstd0_done, 1)
            for g in range(SPANS):
                act.wait_ge(xn_tr, g + 1)
                act.copy(xin[:, 1 + g * WIDE:1 + (g + 1) * WIDE], t0_ps[g % 2]).then_inc(xin0_done, 1)

            with act.Fori(0, A_STEPS) as it:
                after(act, a_qk_done, it + 1)
                act.mul(a_q[:], a_q_ps, A_SCALE).then_inc(a_q_done, 1)
                after(act, a_dif_done, it + 1)
                act.activation(a_p[:], a_dif[:], ACT.Exp).then_inc(a_p_done, 1)
                after(act, a_tp_done, it + 1)
                act.copy(a_pt[:], a_tp[0:4 * PATCH, :]).then_inc(a_pt_done, 1)

            for layer in range(LAYERS):
                if layer:
                    act.preload_act_table_set("natural_log_exp_and_others")

                def norms(n):
                    after(act, qk_ready, n + 1)
                    act.activation(sq[:], qk_ps, ACT.Square).then_inc(sq_done, 1)

                def inverse_norms(n):
                    after(act, ss_done, 2 * n + 2)
                    act.activation(lnss[:], ssc[:], ACT.Ln, scale=LN_SHIFT).then_inc(lnss_done, 1)
                    after(act, lnss_done, n + 1)
                    act.activation(rnorm[:], lnss[:], ACT.Exp, scale=-0.5, bias=eps_s[:, 1:2]).then_inc(rnorm_done, 1)

                def take_v(n, parity):
                    after(act, v_ready, n + 1)
                    after(act, v_off_in, 32 * n)
                    act.copy(v_tok[parity][:], v_ps).then_inc(v_evac, 1)

                def take_qk(n, parity, layers_last=False):
                    after(act, qkt_ready, 2 * n + 1)
                    for h in range(2):
                        rows = slice(64 * h, 64 * h + 64)
                        act.copy(q_diag[parity][rows, :, :, 64 * h:64 * h + 64].rearrange("p c w q -> p (c w) q"),
                                 qk_ps[rows, 0:INNER].rearrange("p (cw q) -> p cw q", q=WINDOW)
                                 ).then_inc(qkt_evac, 1)
                    after(act, qkt_ready, 2 * n + 2)
                    k_new = qk_ps[:, INNER:].rearrange("p (c k) -> p c k", c=CHUNKS)
                    act.copy(k_t[parity][:, :, WINDOW:], k_new).then_inc(qkt_evac, 1)
                    if layers_last:
                        act.memzero(k_t[1 - parity][:, :, 0:WINDOW]).then_inc(qkt_evac, 1)
                    else:
                        act.copy(k_t[1 - parity][:, :, 0:WINDOW], k_new[:, :, WINDOW:]).then_inc(qkt_evac, 1)

                def exps(n, g):
                    after(act, max_done, 2 * n + (g + 1))
                    after(act, probs_n_done, 2 * n + (g - 1))
                    for cw in range(4):
                        k = 4 * g + cw
                        e = act.activation(probs[:, k, :], s_ps[g][:, cw * P:(cw + 1) * P], ACT.Exp,
                                           bias=neg_max[:, k:k + 1], accum_out=row_sum[:, k:k + 1])
                    e.then_inc(probs_done, 1)

                def take_o(n):
                    after(act, ot_ready, n + 1)
                    after(act, y_ready, n)
                    act.copy(o_t[:], ot_ps).then_inc(ot_evac, 1)

                def start(n, t, parity):
                    norms(n)
                    inverse_norms(n)
                    take_v(n, parity)
                    take_qk(n, parity)

                def step(n, t, parity, first, last):
                    exps(n, 0)
                    if not last:
                        norms(n + 1)
                    exps(n, 1)
                    if not last:
                        inverse_norms(n + 1)
                        take_v(n + 1, 1 - parity)
                        take_qk(n + 1, 1 - parity, isinstance(t, int) and t + 2 == TILES)
                    take_o(n)

                over_tiles(act, layer, start, step)

                def variance(j):
                    jj = SPANS * layer + j
                    after(act, cen_ready, jj + 1)
                    act.activation(ln_sq[j % 2][:], cen_ps[j % 2], ACT.Square).then_inc(ln_sq_done, 1)

                variance(0)
                for j in range(SPANS):
                    jj = SPANS * layer + j
                    if j + 1 < SPANS:
                        variance(j + 1)
                    after(act, var_ready, jj + 1)
                    act.activation(ln_log[j % 2][:], var_ps[j % 2], ACT.Ln, bias=eps_s[:, 0:1]).then_inc(ln_log_done, 1)
                    after(act, ln_log_done, jj + 1)
                    after(act, hn_scaled, jj - 1)
                    act.activation(ln_rstd[j % 2][:], ln_log[j % 2][:], ACT.Exp, scale=-0.5).then_inc(ln_rstd_done, 1)

                act.preload_act_table_set("gelu_and_others")
                if layer == 0:
                    act.wait_ge(fw_in, 16 * 6)
                with act.Fori(0, SPANS) as j:
                    jj = j + SPANS * layer
                    for c, (at, size) in enumerate(HID_PARTS):
                        after(act, gate_ready, 3 * jj + (c + 1))
                        after(act, hh_done, 3 * jj if c < 2 else 3 * jj + 1)
                        act.activation(gelu_s[c % 2][0:size, :], gate_ps[c % 2][0:size, :], ACT.Gelu,
                                       bias=b1_s[0:size, layer, 1, c:c + 1]).then_inc(gelu_done, 1)

        @block.vector
        def _(dve):
            dve.wait_ge(x_in, 16)
            for t in range(TILES):
                dve.bn_stats(stats[:, t, :], x_raw[:, t, :]).then_inc(stat_done, 1)
            for t in range(TILES):
                dve.wait_ge(stat_done, t + 1)
                dve.bn_aggr(mv[:, t, :], stats[:, t, :]).then_inc(mv_done, 1)
            dve.wait_ge(rstd0_done, 1)
            for t in range(TILES):
                dve.tensor_scalar(xn_tok[:, t, :], x_raw[:, t, :], mv[:, t, 0:1], rstd0[:, t:t + 1],
                                  ALU.subtract, ALU.mult).then_inc(xn_done, 1)

            dve.wait_ge(const_in, 32)
            dve.tensor_copy(masks[:], masks_f).then_inc(masks_done, 1)

            dve.wait_ge(xin0_done, SPANS)
            with dve.Fori(0, A_STEPS) as it:
                after(dve, a_ot_done, it)
                dve.tensor_copy(a_x[:], xin[:, cols(it * A_STEP + 1, A_WIN)]).then_inc(a_staged, 1)
                after(dve, a_staged, 3 * it + 1)
                for s in range(SHIFT):
                    of = a_x[:, 0:A_STEP].rearrange("p (b i s) -> p b i s", b=2, s=SHIFT)[:, :, :, s]
                    dve.tensor_copy(a_rep[:].rearrange("p (b s) r i -> p b s r i", s=SHIFT)[:, :, s],
                                    of.unsqueeze(2).broadcast_to([P, 2, 4, PATCH])).then_inc(a_staged, 1)
                after(dve, a_qk_done, it + 1)
                dve.tensor_tensor(a_k[:], a_k_ps.unsqueeze(1).broadcast_to([P, 4, A_WIN]),
                                  head_mask.unsqueeze(2).broadcast_to([P, 4, A_WIN]),
                                  ALU.mult).then_inc(a_k_done, 1)
                after(dve, a_vr_done, it + 1)
                dve.tensor_tensor(a_v[:], a_vr[0:4 * PATCH, :].rearrange("p (j d) -> p j d", j=4),
                                  value_mask[0:4 * PATCH, :].unsqueeze(1).broadcast_to([4 * PATCH, 4, DIM]),
                                  ALU.mult).then_inc(a_v_done, 1)
                after(dve, a_s_done, it + 1)
                s4 = a_s.rearrange("p g (h k) -> p g h k", h=4)
                dve.tensor_reduce(a_max[:], s4, AX.X, ALU.max).then_inc(a_max_done, 1)
                after(dve, a_max_done, it + 1)
                dve.tensor_tensor(a_dif[:].rearrange("p (g h) k -> p g h k", g=4), s4,
                                  a_max[:].rearrange("p (g h) -> p g h", g=4).unsqueeze(3)
                                  .broadcast_to([P, 4, 4, PATCH]), ALU.subtract).then_inc(a_dif_done, 1)
                after(dve, a_p_done, it + 1)
                dve.reduce_sum(a_sum[:], a_p[:], AX.X).then_inc(a_sum_done, 1)
                after(dve, a_sum_done, it + 1)
                dve.reciprocal(a_inv[:], a_sum[:]).then_inc(a_inv_done, 1)
                after(dve, a_inv_done, it + 1)
                dve.tensor_tensor(a_pn[:], a_p[:], a_inv[:].unsqueeze(2).broadcast_to([P, A_HEADS, PATCH]),
                                  ALU.mult).then_inc(a_pn_done, 1)
                after(dve, a_op_done, it + 1)
                dve.tensor_copy(a_o[:], a_op[:, 0:DIM]).then_inc(a_o_done, 1)
                after(dve, a_ot_done, it + 1)
                for s in range(SHIFT):
                    to = x_patch[:, cols(it * A_STEP, A_STEP)].rearrange("p (b i s) -> p b i s", b=2, s=SHIFT)
                    of = a_op[:, P:2 * P].rearrange("p (b s i) -> p b s i", b=2, s=SHIFT)
                    o = dve.tensor_copy(to[:, :, :, s], of[:, :, s, 0:PATCH])
                o.then_inc(a_out_done, 1)
            dve.wait_ge(a_out_done, A_STEPS)
            dve.tensor_copy(x_patch[:, PATCHED:N], xin[:, 1 + PATCHED:1 + N]).then_inc(patch_done, 1)

            dve.wait_ge(tab_in, 64)
            for layer in range(LAYERS):
                after(dve, rot_done, 3 * TILES * layer)
                for raw, table in ((cos_raw, cos_w), (sin_raw, sin_w)):
                    for part in range(2):
                        dve.tensor_tensor(table[:, :, part, :], raw[:, :, part, :],
                                          qk_scale[:, layer, part, :].unsqueeze(1).broadcast_to([P, TILES, DH]),
                                          ALU.mult).then_inc(tables_done, 1)
                dve.wait_ge(tables_done, 4 * (layer + 1))

                def sum_squares(n):
                    after(dve, sq_done, n + 1)
                    dve.reduce_sum(ss[:], sq[:].rearrange("p (h d) -> p h d", d=DH), AX.X).then_inc(ss_done, 1)
                    after(dve, ss_done, 2 * n + 1)
                    dve.tensor_scalar(ssc[:], ss[:], NORM_FLOOR_SQ, None, ALU.max).then_inc(ss_done, 1)

                def unit(n):
                    after(dve, rnorm_done, n + 1)
                    after(dve, rot_done, 3 * n)
                    dve.tensor_tensor(qkn[:].rearrange("p (h d) -> p h d", d=DH),
                                      qk_ps.rearrange("p (h d) -> p h d", d=DH),
                                      rnorm[:].unsqueeze(2).broadcast_to([P, 2 * HEADS, DH]),
                                      ALU.mult).then_inc(qkn_done, 1)

                def rotate_cos(n, t):
                    after(dve, qkn_done, n + 1)
                    after(dve, qkt_ready, 2 * n)
                    cos = cos_w[:, cols(t, 1), :, :].rearrange("p a b d -> p (a b) d")
                    dve.tensor_tensor(rot1[:].rearrange("p (a h d) -> p a h d", a=2, d=DH),
                                      qkn[:].rearrange("p (a h d) -> p a h d", a=2, d=DH),
                                      cos.unsqueeze(2).broadcast_to([P, 2, HEADS, DH]),
                                      ALU.mult).then_inc(rot_done, 1)

                def rotate_sin(n, t):
                    for half in range(2):
                        of, to = half * HALF, (1 - half) * HALF
                        sin = sin_w[:, cols(t, 1), :, of:of + HALF].rearrange("p a b d -> p (a b) d")
                        dve.tensor_tensor(rot2[:].rearrange("p (a h d) -> p a h d", a=2, d=DH)[:, :, :, to:to + HALF],
                                          qkn[:].rearrange("p (a h d) -> p a h d", a=2, d=DH)[:, :, :, of:of + HALF],
                                          sin.unsqueeze(2).broadcast_to([P, 2, HEADS, HALF]),
                                          ALU.mult).then_inc(rot_done, 1)

                def maxima(n, g):
                    after(dve, s_ready, 2 * n + (g + 1))
                    dve.tensor_reduce(neg_max[:, 4 * g:4 * g + 4], s_ps[g].rearrange("p (c k) -> p c k", c=4),
                                      AX.X, ALU.max, negate=True).then_inc(max_done, 1)

                def invert(n, g):
                    after(dve, probs_done, 2 * n + (g + 1))
                    dve.reciprocal(row_inv[:, 4 * g:4 * g + 4], row_sum[:, 4 * g:4 * g + 4]).then_inc(inv_done, 1)

                def take_probs(n, g):
                    after(dve, pt_ready, 2 * n + (g + 1))
                    after(dve, ot_ready, n)
                    dve.tensor_copy(probs_t[:, 4 * g:4 * g + 4, :],
                                    s_ps[g].rearrange("p (c k) -> p c k", c=4)).then_inc(pt_evac, 1)

                def residual(n, t):
                    after(dve, y_ready, n + 1)
                    dve.tensor_tensor(x1[:, cols(t * P, P)], y_ps[:, 0:P], xin[:, cols(t * P + 1, P)],
                                      ALU.add).then_inc(x1_done, 1)

                def start(n, t, parity):
                    sum_squares(n)
                    unit(n)
                    rotate_cos(n, t)
                    rotate_sin(n, t)

                def step(n, t, parity, first, last):
                    maxima(n, 0)
                    maxima(n, 1)
                    invert(n, 0)
                    if not last:
                        sum_squares(n + 1)
                    invert(n, 1)
                    take_probs(n, 0)
                    if not last:
                        unit(n + 1)
                    take_probs(n, 1)
                    if not last:
                        rotate_cos(n + 1, t + 1)
                        rotate_sin(n + 1, t + 1)
                    residual(n, t)

                over_tiles(dve, layer, start, step)

                if layer == 0:
                    dve.wait_ge(fw_in, 16 * 6)
                for j in range(SPANS):
                    jj = SPANS * layer + j
                    span = slice(j * WIDE, (j + 1) * WIDE)
                    after(dve, ln_rstd_done, jj + 1)
                    dve.tensor_tensor(hn[:, span], cen_ps[j % 2], ln_rstd[j % 2][:], ALU.mult).then_inc(hn_scaled, 1)
                    after(dve, hn_scaled, jj + 1)
                    dve.tensor_scalar(hn[:, span], hn[:, span], vec_s[:, layer:layer + 1],
                                      vec_s[:, 2 + layer:3 + layer], ALU.mult, ALU.add).then_inc(hn_done, 1)

                if layer == LAYERS - 1:
                    dve.tensor_tensor(b2_out[:], vec_s[:, 5:6], vec_s[:, 6:7], ALU.add).then_inc(tables_done, 1)
                    dve.wait_ge(tables_done, 4 * LAYERS + 1)
                with dve.Fori(0, SPANS) as j:
                    jj = j + SPANS * layer
                    for c, (at, size) in enumerate(HID_PARTS):
                        after(dve, gelu_done, 3 * jj + (c + 1))
                        after(dve, lin_ready, 3 * jj + (c + 1))
                        after(dve, ffn_ready, jj)
                        dve.scalar_tensor_tensor(hh[0:size, c, :], lin_ps[c % 2][0:size, :],
                                                 b1_s[0:size, layer, 0, c:c + 1], gelu_s[c % 2][0:size, :],
                                                 ALU.add, ALU.mult).then_inc(hh_done, 1)
                    after(dve, ffn_ready, jj + 1)
                    if layer < LAYERS - 1:
                        dve.scalar_tensor_tensor(xin[:, cols(j * WIDE + 1, WIDE)], ffn_ps,
                                                 vec_s[:, 4 + layer:5 + layer], x1[:, cols(j * WIDE, WIDE)],
                                                 ALU.add, ALU.add).then_inc(x2_done, 1)
                    else:
                        dve.scalar_tensor_tensor(sum_t[:], ffn_ps, b2_out[:], x1[:, cols(j * WIDE, WIDE)],
                                                 ALU.add, ALU.add).then_inc(x2_done, 1)
                        after(dve, tr_ready, j + 1)
                        after(dve, stored, 16 * j)
                        dve.tensor_tensor(out_s[:], tr_ps,
                                          x_raw[:].rearrange("p t d -> p (t d)")[:, cols(j * WIDE, WIDE)],
                                          ALU.add).then_inc(out_done, 1)


def kernel(**inputs):
    import concourse.bacc as bacc
    from concourse.bass_utils import run_bass_kernel_spmd

    named = {
        "x": inputs["L0_attn_x"],
        "a_wqkv_t": np.transpose(inputs["L0_attn_Wqkv"]),
        "a_wout_t": np.transpose(inputs["L0_attn_Wout"]),
        "wqkv": inputs["L0_ffn_wqkv"],
        "q_scale": inputs["L0_ffn_q_scale"],
        "k_scale": inputs["L0_ffn_k_scale"],
        "wo": inputs["L0_ffn_wo"],
        "w1": inputs["L0_ffn_w1"],
        "w2": inputs["L0_ffn_w2"],
        "vectors": pack_vectors(**{k: inputs["L0_" + k] for k in
                                   ("ffn_b1", "ffn_ln_g", "ffn_ln_b", "ffn_b2", "attn_bout")}),
        **constants(),
    }
    nc = bacc.Bacc("TRN2", target_bir_lowering=False, num_devices=1)
    arrays, args = {}, []
    for name, a in named.items():
        a = np.ascontiguousarray(a)
        arrays[f"in_{name}"] = a
        args.append(nc.dram_tensor(f"in_{name}", a.shape, mybir.dt.from_np(a.dtype), kind="ExternalInput").ap())
    out = nc.dram_tensor("out", (1, N, DIM), F32, kind="ExternalOutput").ap()
    build(nc, *args, out)
    r = run_bass_kernel_spmd(nc, [arrays], core_ids=[0])
    return r.results[0]["out"]
```

```python
from contextlib import ExitStack

import numpy as np

import concourse.bass as bass
import concourse.mybir as mybir
from concourse.alu_op_type import AluOpType as ALU

F32 = mybir.dt.float32
BF16 = mybir.dt.bfloat16
ACT = mybir.ActivationFunctionType
AX = mybir.AxisListType

P = 128
N = 2048
DIM = 128
TILES = N // P
LAYERS = 2
HEADS, DH = 8, 64
HALF = DH // 2
INNER = HEADS * DH
WINDOW = 64
CHUNKS = INNER // P
QK_SCALE = 8.0
HID = int(DIM * 4 * 2 / 3)
HID_PARTS = [(0, 128), (128, 128), (256, HID - 256)]
LN_EPS = 1e-5
WIDE = 512
SPANS = N // WIDE
MASKED = -1e30

PATCH, SHIFT = 20, 2
BLOCK = PATCH * SHIFT
PATCH_BLOCKS = 13
PATCHED = PATCH_BLOCKS * BLOCK
A_HEADS, A_DH = 16, 8
A_SCALE = A_DH ** -0.5
A_STEP = 2 * BLOCK
A_STEPS = -(-PATCHED // A_STEP)
A_WIN = 112
QUADS = 4

LN_SHIFT = 2.0 ** 16
LN_UNSHIFT = float(np.log(2.0 ** 8))
NORM_FLOOR_SQ = 1e-24


def constants():
    half_idx = np.arange(0, DH, 2, dtype=np.float32)
    inv_freq = (1.0 / 10000.0 ** (half_idx / DH)).astype(np.float32)
    t = np.arange(N, dtype=np.float32)
    freqs = (t[:, None] * inv_freq[None, :]).astype(np.float32).astype(np.float64)
    base = (half_idx.astype(np.float64) + 0.4 * DH) / (1.4 * DH)
    scale = base[None, :] ** ((t.astype(np.float64)[:, None] - N // 2) / (WINDOW // 2))
    cos, sin = np.cos(freqs), np.sin(freqs)

    def table(parts):
        full = np.stack([np.concatenate(x, 1) for x in parts], 1).astype(np.float32)
        return np.ascontiguousarray(full.reshape(TILES, P, 2, DH).transpose(1, 0, 2, 3))

    qs, ks = scale * QK_SCALE, 1.0 / scale
    cos_t = table([(cos * qs, cos * qs), (cos * ks, cos * ks)])
    sin_t = table([(sin * qs, -sin * qs), (sin * ks, -sin * ks)])

    ident = np.eye(P, dtype=np.float32)
    i = np.arange(P)[:, None] % WINDOW
    j = np.arange(2 * WINDOW)[None, :]
    usual = np.where((j >= i) & (j <= i + WINDOW), 0.0, MASKED)
    first = np.where((j >= WINDOW) & (j <= i + WINDOW), 0.0, MASKED)
    mask = np.stack([np.tile(usual, (1, 4)), np.concatenate([first, usual] * 2, 1)], 1)
    center = ident - 1.0 / P
    mean = np.full((P, P), 1.0 / P, np.float32)
    head_of = (np.arange(P)[:, None] % 32) // A_DH == np.arange(4)[None, :]
    key_head = np.arange(4 * PATCH) // PATCH
    value_head = (np.arange(P) % 32) // A_DH
    value_mask = np.zeros((P, P), np.float32)
    value_mask[:4 * PATCH] = key_head[:, None] == value_head[None, :]
    small = np.concatenate([ident, center, mean, value_mask, head_of], 1).astype(np.float32)
    masks = np.concatenate([ident, mask.reshape(P, -1)], 1).astype(np.float32)
    return {"cos_t": cos_t, "sin_t": sin_t, "small": small, "masks": masks}


def pack_vectors(ffn_b1, ffn_ln_g, ffn_ln_b, ffn_b2, attn_bout):
    b1 = np.zeros((LAYERS, 2, 3 * P), np.float32)
    b1[:, :, :HID] = np.reshape(ffn_b1, (LAYERS, 2, HID))
    rows = [b1.reshape(12, P), ffn_ln_g, ffn_ln_b, ffn_b2, np.reshape(attn_bout, (1, P))]
    return np.concatenate([np.asarray(r) for r in rows], 0).T


def after(eng, sem, count):
    if not isinstance(count, int) or count > 0:
        eng.wait_ge(sem, count)


def over_tiles(eng, step):
    for t in range(-2, 4):
        step(t, t % 2)
    with eng.Fori(2, TILES // 2 - 1) as i:
        step(i * 2, 0)
        step(i * 2 + 1, 1)
    for t in range(TILES - 2, TILES + 1):
        step(t, t % 2)


def there(t, count=TILES):
    return not isinstance(t, int) or 0 <= t < count


def over_patches(eng, step):
    for t in range(-1, 2):
        step(t)
    with eng.Fori(2, A_STEPS - 1) as t:
        step(t)
    for t in range(A_STEPS - 1, A_STEPS + 1):
        step(t)


def cols(start, size):
    return slice(start, start + size) if isinstance(start, int) else bass.ds(start, size)


def build(nc, x, a_wqkv_t, a_wout_t, wqkv, q_scale, k_scale, wo, w1, w2, vectors_d,
          cos_d, sin_d, small_d, masks_d, out):
    ctx = ExitStack()
    with ctx:
        def sb(name, shape, dt=F32):
            return ctx.enter_context(nc.sbuf_tensor(name, shape, dt))

        def sem(name):
            return ctx.enter_context(nc.semaphore(name))

        small = sb("small", [P, 4 * P + 4])
        ident, center_w, mean_w = small[:, 0:P], small[:, P:2 * P], small[:, 2 * P:3 * P]
        value_mask, head_mask = small[:, 3 * P:4 * P], small[:, 4 * P:4 * P + 4]
        masks = sb("masks", [P, P + 2 * WIDE], BF16)
        ident_bf, usual_mask, first_mask = masks[:, 0:P], masks[:, P:P + WIDE], masks[:, P + WIDE:]
        cos_raw = sb("cos_raw", [P, TILES, 2, DH])
        sin_raw = sb("sin_raw", [P, TILES, 2, DH])
        cos_w = sb("cos_w", [P, TILES, 2, DH])
        sin_w = sb("sin_w", [P, TILES, 2, DH])
        qk_scale = sb("qk_scale", [P, LAYERS, 2, DH])
        a_wqkv_s = sb("a_wqkv_s", [P, 3 * DIM])
        a_wout_s = sb("a_wout_s", [P, DIM])
        wqkv_s = sb("wqkv_s", [P, LAYERS, 3 * INNER])
        wo_s = sb("wo_s", [P, LAYERS, CHUNKS, DIM])
        w1_s = sb("w1_s", [P, LAYERS, 2 * HID])
        w2_s = sb("w2_s", [P, LAYERS, 3, DIM])
        vectors = sb("vectors", [P, 19])
        b1_s = vectors[:, 0:12].rearrange("p (l a c) -> p l a c", l=LAYERS, a=2)
        vec_s = vectors[:, 12:19]
        b2_out = sb("b2_out", [P, 1])
        eps_s = sb("eps_s", [P, 2])

        x_raw = sb("x_raw", [P, TILES, DIM])
        xn_tok = sb("xn_tok", [P, TILES, DIM])
        stats = sb("stats", [P, TILES, 6])
        mv = sb("mv", [P, TILES, 2])
        ln0 = sb("ln0", [P, TILES])
        rstd0 = sb("rstd0", [P, TILES])
        xin = sb("xin", [P, 1 + N])
        x1 = sb("x1", [P, N])
        masks_f = x1[:, 0:P + 2 * WIDE]
        x1_shift = sb("x1_shift", [P, 1 + N])
        x_patch = sb("x_patch", [P, N])
        hn = xn_tok[:].rearrange("p t d -> p (t d)")

        stage = [sb(f"stage{i}", [P, P]) for i in range(2)]
        sq = sb("sq", [P, 2 * INNER])
        ss = sb("ss", [P, 2 * HEADS])
        ssc = sb("ssc", [P, 2 * HEADS])
        lnss = sb("lnss", [P, 2 * HEADS])
        rnorm = sb("rnorm", [P, 2 * HEADS])
        qkn = sb("qkn", [P, 2 * INNER])
        rot1 = sb("rot1", [P, 2 * INNER])
        rot2 = sb("rot2", [P, 2 * INNER])
        q_diag = sb("q_diag", [P, CHUNKS, 2, P])
        k_t = [sb(f"k_t{i}", [P, CHUNKS, WINDOW + P]) for i in range(2)]
        v_tok = [sb(f"v_tok{i}", [P, INNER]) for i in range(2)]
        v_off = [sb(f"v_off{i}", [P, INNER]) for i in range(2)]
        neg_max = sb("neg_max", [P, 8])
        row_sum = sb("row_sum", [P, 8])
        row_inv = sb("row_inv", [P, 8])
        probs = sb("probs", [P, 8, P])
        probs_n = sb("probs_n", [P, 8, P])
        probs_t = sb("probs_t", [P, 8, P])
        o_t = sb("o_t", [P, INNER])

        def halves(tensor):
            return [tensor[:, 0:WIDE], tensor[:, WIDE:2 * WIDE]]

        ln_sq, ln_log, ln_rstd = halves(sq), halves(qkn), halves(rot1)
        gelu_s = halves(rot2)
        hh = probs[:].rearrange("p a k -> p (a k)").rearrange("p (a k) -> p a k", k=WIDE)
        hh = [hh[:, 0, :], hh[:, 1, :], probs_n[:, 0:4, :].rearrange("p a k -> p (a k)")]
        sum_t = probs_n[:, 4:8, :].rearrange("p a k -> p (a k)")
        out_s = o_t

        a_x = sb("a_x", [P, A_WIN])
        a_rep = sb("a_rep", [P, 4, 4, PATCH])
        a_q = sb("a_q", [P, A_WIN])
        a_k = sb("a_k", [P, 4, A_WIN])
        a_v = sb("a_v", [4 * PATCH, 4, DIM])
        a_max = sb("a_max", [P, A_HEADS])
        a_dif = sb("a_dif", [P, A_HEADS, PATCH])
        a_p = sb("a_p", [P, A_HEADS, PATCH])
        a_sum = sb("a_sum", [P, A_HEADS])
        a_inv = sb("a_inv", [P, A_HEADS])
        a_pn = sb("a_pn", [P, A_HEADS, PATCH])
        a_pt = sb("a_pt", [4 * PATCH, WIDE])
        a_o = sb("a_o", [P, DIM])

        ps = ctx.enter_context(nc.psum_tensor("ps", [P, 8 * WIDE], F32))

        def bank(b, n=1):
            return ps[:, b * WIDE:(b + n) * WIDE]

        qk_ps = bank(0, 2)
        v_ps = bank(2)
        s_ps = [bank(3), bank(4)]
        ot_ps = bank(5)
        y_ps = ot_ps
        turn_ps = bank(6, 2)
        cen_ps = [bank(0), bank(1)]
        var_ps = [bank(2), bank(3)]
        gate_ps = [bank(0), bank(1)]
        lin_ps = [bank(2), bank(3)]
        ffn_ps = bank(4)
        tr_ps = bank(5)
        a_s = bank(0, 4).rearrange("p (g c) -> p g c", g=4)[:, :, 0:4 * PATCH]
        a_q_ps = bank(4)[:, 0:A_WIN]
        a_k_ps = bank(5)[:, 0:A_WIN]
        a_vr = bank(6)
        a_tp = bank(4)
        a_op = bank(7)
        t0_ps = [bank(0), bank(1)]

        x_in = sem("x_in")
        const_in = sem("const_in")
        aw_in = sem("aw_in")
        tab_in = sem("tab_in")
        w_in = sem("w_in")
        fw_in = sem("fw_in")
        zeroed = sem("zeroed")
        stat_done = sem("stat_done")
        mv_done = sem("mv_done")
        ln0_done = sem("ln0_done")
        rstd0_done = sem("rstd0_done")
        xn_done = sem("xn_done")
        xn_tr = sem("xn_tr")
        xin0_done = sem("xin0_done")
        a_staged = sem("a_staged")
        a_qk_done = sem("a_qk_done")
        a_vr_done = sem("a_vr_done")
        a_q_done = sem("a_q_done")
        a_k_done = sem("a_k_done")
        a_v_done = sem("a_v_done")
        a_s_done = sem("a_s_done")
        a_max_done = sem("a_max_done")
        a_dif_done = sem("a_dif_done")
        a_p_done = sem("a_p_done")
        a_sum_done = sem("a_sum_done")
        a_inv_done = sem("a_inv_done")
        a_pn_done = sem("a_pn_done")
        a_tp_done = sem("a_tp_done")
        a_pt_done = sem("a_pt_done")
        a_op_done = sem("a_op_done")
        a_o_done = sem("a_o_done")
        a_ot_done = sem("a_ot_done")
        a_out_done = sem("a_out_done")
        patch_done = sem("patch_done")
        tables_done = sem("tables_done")
        masks_done = sem("masks_done")
        staged = sem("staged")
        qk_ready = sem("qk_ready")
        v_ready = sem("v_ready")
        sq_done = sem("sq_done")
        ss_done = sem("ss_done")
        lnss_done = sem("lnss_done")
        rnorm_done = sem("rnorm_done")
        qkn_done = sem("qkn_done")
        rot_done = sem("rot_done")
        qkt_ready = sem("qkt_ready")
        qkt_evac = sem("qkt_evac")
        v_evac = sem("v_evac")
        v_off_in = sem("v_off_in")
        s_ready = sem("s_ready")
        max_done = sem("max_done")
        probs_done = sem("probs_done")
        inv_done = sem("inv_done")
        probs_n_done = sem("probs_n_done")
        pt_ready = sem("pt_ready")
        pt_evac = sem("pt_evac")
        ot_ready = sem("ot_ready")
        ot_evac = sem("ot_evac")
        y_ready = sem("y_ready")
        x1_done = sem("x1_done")
        x1_shifted = sem("x1_shifted")
        cen_ready = sem("cen_ready")
        ln_sq_done = sem("ln_sq_done")
        var_ready = sem("var_ready")
        ln_log_done = sem("ln_log_done")
        ln_rstd_done = sem("ln_rstd_done")
        hn_scaled = sem("hn_scaled")
        hn_done = sem("hn_done")
        gate_ready = sem("gate_ready")
        lin_ready = sem("lin_ready")
        gelu_done = sem("gelu_done")
        hh_done = sem("hh_done")
        ffn_ready = sem("ffn_ready")
        x2_done = sem("x2_done")
        tr_ready = sem("tr_ready")
        out_done = sem("out_done")
        stored = sem("stored")

        block = ctx.enter_context(nc.Block())

        @block.sync
        def _(sp):
            sp.dma_start(x_raw[:], x.rearrange("a (t p) d -> p (a t) d", p=P)).then_inc(x_in, 16)
            sp.dma_start(small[:], small_d).then_inc(const_in, 16)
            sp.dma_start(masks_f, masks_d).then_inc(const_in, 16)
            sp.dma_start(a_wqkv_s[:], a_wqkv_t).then_inc(aw_in, 16)
            sp.dma_start(cos_raw[:], cos_d).then_inc(tab_in, 16)
            sp.dma_start(sin_raw[:], sin_d).then_inc(tab_in, 16)
            for part, scale in enumerate((q_scale, k_scale)):
                sp.dma_start(qk_scale[:, :, part, :], scale.partition_broadcast(P)).then_inc(tab_in, 16)
            sp.dma_start(wqkv_s[:], wqkv.rearrange("l p n -> p l n")).then_inc(w_in, 16)
            sp.dma_start(wo_s[:], wo.rearrange("l (c p) n -> p l c n", p=P)).then_inc(w_in, 16)
            sp.dma_start(w1_s[:], w1.rearrange("l p n -> p l n")).then_inc(fw_in, 16)
            sp.dma_start(a_wout_s[:], a_wout_t).then_inc(fw_in, 16)
            for c, (at, size) in enumerate(HID_PARTS):
                sp.dma_start(w2_s[0:size, :, c, :],
                             w2[:, at:at + size, :].rearrange("l p n -> p l n")).then_inc(fw_in, 16)
            sp.dma_start(vectors[:], vectors_d).then_inc(fw_in, 16)

            def shift_values(n, parity):
                after(sp, v_evac, n + 1)
                sp.dma_start(v_off[parity][0:WINDOW, :], v_tok[1 - parity][WINDOW:P, :]).then_inc(v_off_in, 16)
                sp.dma_start(v_off[parity][WINDOW:P, :], v_tok[parity][0:WINDOW, :]).then_inc(v_off_in, 16)

            sp.wait_ge(zeroed, 5)
            for layer in range(LAYERS):
                def step(t, parity):
                    if there(t):
                        shift_values(t + layer * TILES, parity)

                over_tiles(sp, step)
            for j in range(SPANS):
                sp.wait_ge(out_done, j + 1)
                sp.dma_start(out[0, cols(j * WIDE, WIDE), :].rearrange("(q p) d -> p q d", p=P),
                             out_s[:].rearrange("p (q d) -> p q d", q=4)).then_inc(stored, 16)
            sp.wait_ge(stored, 16 * SPANS)

        @block.gpsimd
        def _(pool):
            pool.memset(xin[:, 0:1], 0.0).then_inc(zeroed, 1)
            pool.memset(x1_shift[:, 0:1], 0.0).then_inc(zeroed, 1)
            pool.memset(v_tok[1][:], 0.0).then_inc(zeroed, 1)
            pool.memset(k_t[0][:], 0.0).then_inc(zeroed, 1)
            pool.memset(eps_s[:, 0:1], LN_EPS).then_inc(zeroed, 1)
            pool.memset(eps_s[:, 1:2], LN_UNSHIFT).then_inc(zeroed, 1)
            pool.memset(q_diag[:], 0.0).then_inc(zeroed, 1)

            def make_stage(n, t, parity):
                after(pool, probs_n_done, 2 * n - 4)
                after(pool, v_ready, n - 1)
                pool.tensor_copy(stage[parity][0:64, :], xin[0:64, cols(t * P + 1, P)]).then_inc(staged, 1)
                pool.tensor_copy(stage[parity][64:P, :], xin[64:P, cols(t * P, P)]).then_inc(staged, 1)

            def normalize(n, g, ended):
                after(pool, staged, ended)
                after(pool, x1_shifted, 2 * n - 4)
                after(pool, inv_done, 2 * n + (g + 1))
                after(pool, pt_ready, 2 * n + (g - 1))
                pool.tensor_tensor(probs_n[:, 4 * g:4 * g + 4, :], probs[:, 4 * g:4 * g + 4, :],
                                   row_inv[:, 4 * g:4 * g + 4].unsqueeze(2).broadcast_to([P, 4, P]),
                                   ALU.mult).then_inc(probs_n_done, 1)

            def shift_x1(n, t, ended):
                after(pool, probs_n_done, ended)
                after(pool, x1_done, n + 1)
                pool.tensor_copy(x1_shift[0:64, cols(t * P, P)], x1[0:64, cols(t * P, P)]).then_inc(x1_shifted, 1)
                pool.tensor_copy(x1_shift[64:P, cols(t * P + 1, P)], x1[64:P, cols(t * P, P)]).then_inc(x1_shifted, 1)

            for layer in range(LAYERS):
                if layer == 0:
                    pool.wait_ge(xin0_done, SPANS)
                else:
                    pool.wait_ge(x2_done, SPANS)
                n0 = layer * TILES

                def step(t, parity):
                    n = t + n0
                    if there(t + 2):
                        make_stage(n + 2, t + 2, parity)
                    if there(t):
                        for g in range(2):
                            normalize(n, g, 2 * n + 6 if there(t + 2) else 2 * (n0 + TILES))
                    if there(t - 2):
                        shift_x1(n - 2, t - 2, 2 * n + 2 if there(t) else 2 * n)

                over_tiles(pool, step)
                shift_x1(n0 + TILES - 1, TILES - 1, 2 * (n0 + TILES))

        @block.tensor
        def _(pe):
            pe.wait_ge(const_in, 32)
            for g in range(SPANS):
                pe.wait_ge(xn_done, 4 * g + 4)
                if g >= 2:
                    pe.wait_ge(xin0_done, g - 1)
                for q in range(4):
                    mm = pe.transpose(t0_ps[g % 2][:, q * P:(q + 1) * P], xn_tok[:, 4 * g + q, :], ident)
                mm.then_inc(xn_tr, 1)

            pe.wait_ge(aw_in, 16)
            pe.wait_ge(xin0_done, SPANS)

            def turn_patch_probs(t):
                after(pe, a_pn_done, t + 1)
                for g in range(QUADS):
                    mm = pe.transpose(a_tp[0:4 * PATCH, g * P:(g + 1) * P],
                                      a_pn[:, 4 * g:4 * g + 4, :].rearrange("p h k -> p (h k)"), ident)
                mm.then_inc(a_tp_done, 1)

            def patch_scores(t):
                for j in range(4):
                    at = BLOCK * (j // 2) + j % 2
                    for g in range(QUADS):
                        mm = pe.matmul(a_s[32 * j:32 * j + 32, g, :],
                                       a_q[32 * g:32 * g + 32, at:at + 63:SHIFT],
                                       a_k[32 * g:32 * g + 32, :, at:at + BLOCK - 1:SHIFT],
                                       start=True, stop=True)
                mm.then_inc(a_s_done, 1)

            def weigh_patch_values(t):
                after(pe, a_pt_done, t + 1)
                after(pe, a_v_done, t + 1)
                after(pe, a_out_done, t)
                for j in range(4):
                    for g in range(QUADS):
                        mm = pe.matmul(a_op[32 * j:32 * j + 32, 32 * g:32 * g + 32],
                                       a_pt[:, g * P + 32 * j:g * P + 32 * j + 32],
                                       a_v[:, j, 32 * g:32 * g + 32], start=True, stop=True)
                mm.then_inc(a_op_done, 1)

            def project_patch_qk(t):
                after(pe, a_staged, 3 * t + 3)
                after(pe, a_k_done, t)
                after(pe, a_pt_done, t - 1)
                pe.matmul(a_q_ps, a_wqkv_s[:, 0:DIM], a_x[:], start=True, stop=True)
                pe.matmul(a_k_ps, a_wqkv_s[:, DIM:2 * DIM], a_x[:],
                          start=True, stop=True).then_inc(a_qk_done, 1)

            def project_patch_values(t):
                after(pe, a_v_done, t)
                for j in range(4):
                    mm = pe.matmul(a_vr[0:4 * PATCH, j * DIM:(j + 1) * DIM],
                                   a_rep[:, j, :, :].rearrange("p r i -> p (r i)"),
                                   a_wqkv_s[:, 2 * DIM:3 * DIM], start=True, stop=True)
                mm.then_inc(a_vr_done, 1)

            def patch_step(t):
                if there(t, A_STEPS):
                    after(pe, a_q_done, t + 1)
                    after(pe, a_k_done, t + 1)
                    after(pe, a_dif_done, t)
                if there(t - 1, A_STEPS):
                    turn_patch_probs(t - 1)
                if there(t, A_STEPS):
                    patch_scores(t)
                if there(t - 1, A_STEPS):
                    weigh_patch_values(t - 1)
                if there(t + 1, A_STEPS):
                    project_patch_qk(t + 1)
                    project_patch_values(t + 1)
                if there(t - 1, A_STEPS):
                    after(pe, a_o_done, t)
                    pe.transpose(a_op[:, P:2 * P], a_o[:], ident).then_inc(a_ot_done, 1)

            over_patches(pe, patch_step)
            pe.wait_ge(a_out_done, A_STEPS)

            pe.wait_ge(w_in, 32)
            pe.wait_ge(masks_done, 1)
            for layer in range(LAYERS):
                def project_qk(n, parity):
                    after(pe, staged, 2 * n + 2)
                    after(pe, qkn_done, n)
                    pe.matmul(qk_ps[:, 0:INNER], stage[parity][:], wqkv_s[:, layer, 0:INNER],
                              start=True, stop=True)
                    pe.matmul(qk_ps[:, INNER:], stage[parity][:], wqkv_s[:, layer, INNER:2 * INNER],
                              start=True, stop=True).then_inc(qk_ready, 1)

                def project_v(n, parity):
                    after(pe, v_evac, n)
                    pe.matmul(v_ps, stage[parity][:], wqkv_s[:, layer, 2 * INNER:],
                              start=True, stop=True).then_inc(v_ready, 1)

                def turn(n):
                    after(pe, rot_done, 3 * n + 3)
                    after(pe, qkt_evac, 4 * n)
                    for part in range(2):
                        for c in range(CHUNKS):
                            at = part * INNER + c * P
                            pe.matmul(turn_ps[:, at:at + P], rot1[:, at:at + P], ident,
                                      start=True, stop=False, is_transpose=True)
                            mm = pe.matmul(turn_ps[:, at:at + P], rot2[:, at:at + P], ident,
                                           start=False, stop=True, is_transpose=True)
                        mm.then_inc(qkt_ready, 1)

                def scores(n, parity, g, mask):
                    after(pe, qkt_evac, 4 * n + 4)
                    after(pe, pt_evac, 2 * n + (g - 1))
                    pe.matmul(s_ps[g], ident_bf, mask, start=True, stop=False, skip_group_check=True)
                    for cw in range(4):
                        c, w = 2 * g + cw // 2, cw % 2
                        mm = pe.matmul(s_ps[g][:, cw * P:(cw + 1) * P], q_diag[:, c, w, :],
                                       k_t[parity][:, c, w * WINDOW:w * WINDOW + P],
                                       start=False, stop=True, skip_group_check=True)
                    mm.then_inc(s_ready, 1)

                def turn_probs(n, g):
                    after(pe, probs_n_done, 2 * n + (g + 1))
                    for cw in range(4):
                        mm = pe.transpose(s_ps[g][:, cw * P:(cw + 1) * P], probs_n[:, 4 * g + cw, :], ident)
                    mm.then_inc(pt_ready, 1)

                def weigh_values(n, parity):
                    after(pe, pt_evac, 2 * n + 2)
                    after(pe, v_off_in, 32 * n + 32)
                    after(pe, x1_done, n)
                    for c in range(CHUNKS):
                        for w in range(2):
                            v = (v_off if w == 0 else v_tok)[parity]
                            for h in range(2):
                                head = (2 * c + h) * DH
                                mm = pe.matmul(ot_ps[64 * h:64 * h + 64, c * P + w * WINDOW:c * P + (w + 1) * WINDOW],
                                               v[:, head:head + DH],
                                               probs_t[:, 2 * c + w, h * WINDOW:(h + 1) * WINDOW],
                                               start=True, stop=True)
                    mm.then_inc(ot_ready, 1)

                def project_out(n):
                    after(pe, ot_evac, n + 1)
                    for c in range(CHUNKS):
                        mm = pe.matmul(y_ps[:, 0:P], wo_s[:, layer, c, :], o_t[:, c * P:(c + 1) * P],
                                       start=(c == 0), stop=(c == CHUNKS - 1))
                    mm.then_inc(y_ready, 1)

                def step(t, parity):
                    n = t + layer * TILES
                    if there(t):
                        mask = first_mask if isinstance(t, int) and t == 0 else usual_mask
                        scores(n, parity, 0, mask)
                        scores(n, parity, 1, mask)
                    if there(t + 2):
                        project_qk(n + 2, parity)
                    if there(t - 1):
                        weigh_values(n - 1, 1 - parity)
                    if there(t + 1):
                        turn(n + 1)
                    if there(t):
                        turn_probs(n, 0)
                        turn_probs(n, 1)
                    if there(t + 1):
                        project_v(n + 1, 1 - parity)
                    if there(t - 1):
                        project_out(n - 1)

                over_tiles(pe, step)

                pe.wait_ge(x1_shifted, 2 * TILES * (layer + 1))

                def centered(j):
                    jj = SPANS * layer + j
                    after(pe, hn_scaled, jj - 1)
                    pe.matmul(cen_ps[j % 2], center_w, x1_shift[:, j * WIDE:(j + 1) * WIDE],
                              start=True, stop=True).then_inc(cen_ready, 1)

                centered(0)
                for j in range(SPANS):
                    jj = SPANS * layer + j
                    if j + 1 < SPANS:
                        centered(j + 1)
                    after(pe, ln_sq_done, jj + 1)
                    after(pe, ln_log_done, jj - 1)
                    pe.matmul(var_ps[j % 2], mean_w, ln_sq[j % 2], start=True, stop=True).then_inc(var_ready, 1)

                if layer == 0:
                    pe.wait_ge(fw_in, 16 * 6)
                pe.wait_ge(hn_done, SPANS * (layer + 1))
                if layer == LAYERS - 1:
                    pe.wait_ge(patch_done, 1)
                with pe.Fori(0, SPANS) as j:
                    jj = j + SPANS * layer
                    for c, (at, size) in enumerate(HID_PARTS):
                        after(pe, hh_done, 3 * jj if c < 2 else 3 * jj + 1)
                        pe.matmul(gate_ps[c % 2][0:size, :], w1_s[:, layer, HID + at:HID + at + size],
                                  hn[:, cols(j * WIDE, WIDE)], start=True, stop=True).then_inc(gate_ready, 1)
                        pe.matmul(lin_ps[c % 2][0:size, :], w1_s[:, layer, at:at + size],
                                  hn[:, cols(j * WIDE, WIDE)], start=True, stop=True).then_inc(lin_ready, 1)
                    after(pe, x2_done, jj)
                    if layer == LAYERS - 1:
                        pe.matmul(ffn_ps, a_wout_s[:], x_patch[:, cols(j * WIDE, WIDE)], start=True, stop=False)
                    for c, (at, size) in enumerate(HID_PARTS):
                        after(pe, hh_done, 3 * jj + (c + 1))
                        mm = pe.matmul(ffn_ps, w2_s[0:size, layer, c, :], hh[c][0:size, :],
                                       start=(c == 0 and layer < LAYERS - 1), stop=(c == 2))
                    mm.then_inc(ffn_ready, 1)
                    if layer == LAYERS - 1:
                        after(pe, x2_done, jj + 1)
                        after(pe, out_done, j)
                        for q in range(4):
                            mm = pe.transpose(tr_ps[:, q * P:(q + 1) * P], sum_t[:, q * P:(q + 1) * P], ident)
                        mm.then_inc(tr_ready, 1)

        @block.scalar
        def _(act):
            act.preload_act_table_set("natural_log_exp_and_others")
            act.wait_ge(zeroed, 7)
            act.wait_ge(mv_done, TILES)
            act.activation(ln0[:], mv[:, :, 1], ACT.Ln, bias=eps_s[:, 0:1]).then_inc(ln0_done, 1)
            act.wait_ge(ln0_done, 1)
            act.activation(rstd0[:], ln0[:], ACT.Exp, scale=-0.5).then_inc(rstd0_done, 1)
            for g in range(SPANS):
                act.wait_ge(xn_tr, g + 1)
                act.copy(xin[:, 1 + g * WIDE:1 + (g + 1) * WIDE], t0_ps[g % 2]).then_inc(xin0_done, 1)

            def patch_step(t):
                if there(t - 1, A_STEPS):
                    after(act, a_tp_done, t)
                    after(act, a_op_done, t - 1)
                    act.copy(a_pt[:], a_tp[0:4 * PATCH, :]).then_inc(a_pt_done, 1)
                if there(t, A_STEPS):
                    after(act, a_dif_done, t + 1)
                    act.activation(a_p[:], a_dif[:], ACT.Exp).then_inc(a_p_done, 1)
                if there(t + 1, A_STEPS):
                    after(act, a_qk_done, t + 2)
                    after(act, a_s_done, t + 1)
                    act.mul(a_q[:], a_q_ps, A_SCALE).then_inc(a_q_done, 1)

            over_patches(act, patch_step)

            for layer in range(LAYERS):
                if layer:
                    act.preload_act_table_set("natural_log_exp_and_others")

                def norms(n):
                    after(act, qk_ready, n + 1)
                    act.activation(sq[:], qk_ps, ACT.Square).then_inc(sq_done, 1)

                def inverse_norms(n):
                    after(act, ss_done, 2 * n + 2)
                    act.activation(lnss[:], ssc[:], ACT.Ln, scale=LN_SHIFT).then_inc(lnss_done, 1)
                    after(act, lnss_done, n + 1)
                    act.activation(rnorm[:], lnss[:], ACT.Exp, scale=-0.5, bias=eps_s[:, 1:2]).then_inc(rnorm_done, 1)

                def take_v(n, parity):
                    after(act, v_ready, n + 1)
                    after(act, v_off_in, 32 * n)
                    act.copy(v_tok[parity][:], v_ps).then_inc(v_evac, 1)

                def take_q(n):
                    after(act, qkt_ready, 2 * n + 1)
                    for h in range(2):
                        rows = slice(64 * h, 64 * h + 64)
                        act.copy(q_diag[rows, :, :, 64 * h:64 * h + 64].rearrange("p c w q -> p (c w) q"),
                                 turn_ps[rows, 0:INNER].rearrange("p (cw q) -> p cw q", q=WINDOW)
                                 ).then_inc(qkt_evac, 1)

                def take_k(n, parity, layers_last):
                    after(act, qkt_ready, 2 * n + 2)
                    k_new = turn_ps[:, INNER:].rearrange("p (c k) -> p c k", c=CHUNKS)
                    act.copy(k_t[parity][:, :, WINDOW:], k_new).then_inc(qkt_evac, 1)
                    if layers_last:
                        act.memzero(k_t[1 - parity][:, :, 0:WINDOW]).then_inc(qkt_evac, 1)
                    else:
                        act.copy(k_t[1 - parity][:, :, 0:WINDOW], k_new[:, :, WINDOW:]).then_inc(qkt_evac, 1)

                def exps(n, g):
                    after(act, max_done, 2 * n + (g + 1))
                    after(act, probs_n_done, 2 * n + (g - 1))
                    for cw in range(4):
                        k = 4 * g + cw
                        e = act.activation(probs[:, k, :], s_ps[g][:, cw * P:(cw + 1) * P], ACT.Exp,
                                           bias=neg_max[:, k:k + 1], accum_out=row_sum[:, k:k + 1])
                    e.then_inc(probs_done, 1)

                def take_o(n):
                    after(act, ot_ready, n + 1)
                    after(act, y_ready, n)
                    act.copy(o_t[:], ot_ps).then_inc(ot_evac, 1)

                def step(t, parity):
                    n = t + layer * TILES
                    if there(t):
                        exps(n, 0)
                        exps(n, 1)
                    if there(t + 2):
                        norms(n + 2)
                    if there(t - 1):
                        take_o(n - 1)
                    if there(t + 1):
                        take_q(n + 1)
                        take_k(n + 1, 1 - parity, isinstance(t, int) and t + 2 == TILES)
                    if there(t + 2):
                        inverse_norms(n + 2)
                    if there(t + 1):
                        take_v(n + 1, 1 - parity)

                over_tiles(act, step)

                def variance(j):
                    jj = SPANS * layer + j
                    after(act, cen_ready, jj + 1)
                    act.activation(ln_sq[j % 2], cen_ps[j % 2], ACT.Square).then_inc(ln_sq_done, 1)

                variance(0)
                for j in range(SPANS):
                    jj = SPANS * layer + j
                    if j + 1 < SPANS:
                        variance(j + 1)
                    after(act, var_ready, jj + 1)
                    act.activation(ln_log[j % 2], var_ps[j % 2], ACT.Ln, bias=eps_s[:, 0:1]).then_inc(ln_log_done, 1)
                    after(act, ln_log_done, jj + 1)
                    after(act, hn_scaled, jj - 1)
                    act.activation(ln_rstd[j % 2], ln_log[j % 2], ACT.Exp, scale=-0.5).then_inc(ln_rstd_done, 1)

                act.preload_act_table_set("gelu_and_others")
                if layer == 0:
                    act.wait_ge(fw_in, 16 * 6)
                with act.Fori(0, SPANS) as j:
                    jj = j + SPANS * layer
                    for c, (at, size) in enumerate(HID_PARTS):
                        after(act, gate_ready, 3 * jj + (c + 1))
                        after(act, hh_done, 3 * jj if c < 2 else 3 * jj + 1)
                        act.activation(gelu_s[c % 2][0:size, :], gate_ps[c % 2][0:size, :], ACT.Gelu,
                                       bias=b1_s[0:size, layer, 1, c:c + 1]).then_inc(gelu_done, 1)

        @block.vector
        def _(dve):
            dve.wait_ge(x_in, 16)
            for t in range(TILES):
                dve.bn_stats(stats[:, t, :], x_raw[:, t, :]).then_inc(stat_done, 1)
            for t in range(TILES):
                dve.wait_ge(stat_done, t + 1)
                dve.bn_aggr(mv[:, t, :], stats[:, t, :]).then_inc(mv_done, 1)
            dve.wait_ge(rstd0_done, 1)
            for t in range(TILES):
                dve.tensor_scalar(xn_tok[:, t, :], x_raw[:, t, :], mv[:, t, 0:1], rstd0[:, t:t + 1],
                                  ALU.subtract, ALU.mult).then_inc(xn_done, 1)

            dve.wait_ge(const_in, 32)
            dve.tensor_copy(masks[:], masks_f).then_inc(masks_done, 1)

            dve.wait_ge(xin0_done, SPANS)

            def stage_patches(t):
                after(dve, a_vr_done, t)
                dve.tensor_copy(a_x[:], xin[:, cols(t * A_STEP + 1, A_WIN)]).then_inc(a_staged, 1)
                after(dve, a_staged, 3 * t + 1)
                for s in range(SHIFT):
                    of = a_x[:, 0:A_STEP].rearrange("p (b i s) -> p b i s", b=2, s=SHIFT)[:, :, :, s]
                    dve.tensor_copy(a_rep[:].rearrange("p (b s) r i -> p b s r i", s=SHIFT)[:, :, s],
                                    of.unsqueeze(2).broadcast_to([P, 2, 4, PATCH])).then_inc(a_staged, 1)

            def patch_keys(t):
                after(dve, a_qk_done, t + 1)
                after(dve, a_s_done, t)
                dve.tensor_tensor(a_k[:], a_k_ps.unsqueeze(1).broadcast_to([P, 4, A_WIN]),
                                  head_mask.unsqueeze(2).broadcast_to([P, 4, A_WIN]),
                                  ALU.mult).then_inc(a_k_done, 1)

            def patch_values(t):
                after(dve, a_vr_done, t + 1)
                after(dve, a_op_done, t)
                dve.tensor_tensor(a_v[:], a_vr[0:4 * PATCH, :].rearrange("p (j d) -> p j d", j=4),
                                  value_mask[0:4 * PATCH, :].unsqueeze(1).broadcast_to([4 * PATCH, 4, DIM]),
                                  ALU.mult).then_inc(a_v_done, 1)

            def patch_differences(t):
                s4 = a_s.rearrange("p g (h k) -> p g h k", h=4)
                after(dve, a_s_done, t + 1)
                dve.tensor_reduce(a_max[:], s4, AX.X, ALU.max).then_inc(a_max_done, 1)
                after(dve, a_max_done, t + 1)
                after(dve, a_p_done, t)
                dve.tensor_tensor(a_dif[:].rearrange("p (g h) k -> p g h k", g=4), s4,
                                  a_max[:].rearrange("p (g h) -> p g h", g=4).unsqueeze(3)
                                  .broadcast_to([P, 4, 4, PATCH]), ALU.subtract).then_inc(a_dif_done, 1)

            def patch_step(t):
                if there(t + 1, A_STEPS):
                    stage_patches(t + 1)
                if there(t, A_STEPS):
                    patch_differences(t)
                    after(dve, a_p_done, t + 1)
                    dve.reduce_sum(a_sum[:], a_p[:], AX.X).then_inc(a_sum_done, 1)
                    after(dve, a_sum_done, t + 1)
                    dve.reciprocal(a_inv[:], a_sum[:]).then_inc(a_inv_done, 1)
                if there(t - 1, A_STEPS):
                    after(dve, a_op_done, t)
                    dve.tensor_copy(a_o[:], a_op[:, 0:DIM]).then_inc(a_o_done, 1)
                if not there(t, A_STEPS) and there(t + 1, A_STEPS):
                    patch_keys(0)
                if there(t, A_STEPS):
                    patch_values(t)
                    if there(t + 1, A_STEPS):
                        patch_keys(t + 1)
                    after(dve, a_inv_done, t + 1)
                    after(dve, a_tp_done, t)
                    dve.tensor_tensor(a_pn[:], a_p[:], a_inv[:].unsqueeze(2).broadcast_to([P, A_HEADS, PATCH]),
                                      ALU.mult).then_inc(a_pn_done, 1)
                if there(t - 1, A_STEPS):
                    after(dve, a_ot_done, t)
                    for s in range(SHIFT):
                        to = x_patch[:, cols((t - 1) * A_STEP, A_STEP)].rearrange("p (b i s) -> p b i s", b=2, s=SHIFT)
                        of = a_op[:, P:2 * P].rearrange("p (b s i) -> p b s i", b=2, s=SHIFT)
                        o = dve.tensor_copy(to[:, :, :, s], of[:, :, s, 0:PATCH])
                    o.then_inc(a_out_done, 1)

            over_patches(dve, patch_step)
            dve.wait_ge(a_out_done, A_STEPS)
            dve.tensor_copy(x_patch[:, PATCHED:N], xin[:, 1 + PATCHED:1 + N]).then_inc(patch_done, 1)

            dve.wait_ge(tab_in, 64)
            for layer in range(LAYERS):
                after(dve, rot_done, 3 * TILES * layer)
                for raw, table in ((cos_raw, cos_w), (sin_raw, sin_w)):
                    for part in range(2):
                        dve.tensor_tensor(table[:, :, part, :], raw[:, :, part, :],
                                          qk_scale[:, layer, part, :].unsqueeze(1).broadcast_to([P, TILES, DH]),
                                          ALU.mult).then_inc(tables_done, 1)
                dve.wait_ge(tables_done, 4 * (layer + 1))

                def sum_squares(n):
                    after(dve, sq_done, n + 1)
                    dve.reduce_sum(ss[:], sq[:].rearrange("p (h d) -> p h d", d=DH), AX.X).then_inc(ss_done, 1)
                    after(dve, ss_done, 2 * n + 1)
                    dve.tensor_scalar(ssc[:], ss[:], NORM_FLOOR_SQ, None, ALU.max).then_inc(ss_done, 1)

                def unit(n):
                    after(dve, rnorm_done, n + 1)
                    after(dve, rot_done, 3 * n)
                    dve.tensor_tensor(qkn[:].rearrange("p (h d) -> p h d", d=DH),
                                      qk_ps.rearrange("p (h d) -> p h d", d=DH),
                                      rnorm[:].unsqueeze(2).broadcast_to([P, 2 * HEADS, DH]),
                                      ALU.mult).then_inc(qkn_done, 1)

                def rotate_cos(n, t):
                    cos = cos_w[:, cols(t, 1), :, :].rearrange("p a b d -> p (a b) d")
                    dve.tensor_tensor(rot1[:].rearrange("p (a h d) -> p a h d", a=2, d=DH),
                                      qkn[:].rearrange("p (a h d) -> p a h d", a=2, d=DH),
                                      cos.unsqueeze(2).broadcast_to([P, 2, HEADS, DH]),
                                      ALU.mult).then_inc(rot_done, 1)

                def rotate_sin(n, t, half):
                    after(dve, qkn_done, n + 1)
                    after(dve, qkt_ready, 2 * n)
                    of, to = half * HALF, (1 - half) * HALF
                    sin = sin_w[:, cols(t, 1), :, of:of + HALF].rearrange("p a b d -> p (a b) d")
                    dve.tensor_tensor(rot2[:].rearrange("p (a h d) -> p a h d", a=2, d=DH)[:, :, :, to:to + HALF],
                                      qkn[:].rearrange("p (a h d) -> p a h d", a=2, d=DH)[:, :, :, of:of + HALF],
                                      sin.unsqueeze(2).broadcast_to([P, 2, HEADS, HALF]),
                                      ALU.mult).then_inc(rot_done, 1)

                def maxima(n, g):
                    after(dve, s_ready, 2 * n + (g + 1))
                    dve.tensor_reduce(neg_max[:, 4 * g:4 * g + 4], s_ps[g].rearrange("p (c k) -> p c k", c=4),
                                      AX.X, ALU.max, negate=True).then_inc(max_done, 1)

                def invert(n, g):
                    after(dve, probs_done, 2 * n + (g + 1))
                    dve.reciprocal(row_inv[:, 4 * g:4 * g + 4], row_sum[:, 4 * g:4 * g + 4]).then_inc(inv_done, 1)

                def take_probs(n, g):
                    after(dve, pt_ready, 2 * n + (g + 1))
                    dve.tensor_copy(probs_t[:, 4 * g:4 * g + 4, :],
                                    s_ps[g].rearrange("p (c k) -> p c k", c=4)).then_inc(pt_evac, 1)

                def residual(n, t):
                    after(dve, y_ready, n + 1)
                    dve.tensor_tensor(x1[:, cols(t * P, P)], y_ps[:, 0:P], xin[:, cols(t * P + 1, P)],
                                      ALU.add).then_inc(x1_done, 1)

                def step(t, parity):
                    n = t + layer * TILES
                    if there(t):
                        maxima(n, 0)
                    if there(t + 1):
                        rotate_sin(n + 1, t + 1, 0)
                    if there(t):
                        maxima(n, 1)
                    if there(t + 1):
                        rotate_sin(n + 1, t + 1, 1)
                        rotate_cos(n + 1, t + 1)
                    if there(t):
                        invert(n, 0)
                        invert(n, 1)
                    if there(t + 2):
                        sum_squares(n + 2)
                    if there(t):
                        take_probs(n, 0)
                        take_probs(n, 1)
                    if there(t + 2):
                        unit(n + 2)
                    if there(t - 1):
                        residual(n - 1, t - 1)

                over_tiles(dve, step)

                if layer == 0:
                    dve.wait_ge(fw_in, 16 * 6)
                for j in range(SPANS):
                    jj = SPANS * layer + j
                    span = slice(j * WIDE, (j + 1) * WIDE)
                    after(dve, ln_rstd_done, jj + 1)
                    dve.tensor_tensor(hn[:, span], cen_ps[j % 2], ln_rstd[j % 2], ALU.mult).then_inc(hn_scaled, 1)
                    after(dve, hn_scaled, jj + 1)
                    dve.tensor_scalar(hn[:, span], hn[:, span], vec_s[:, layer:layer + 1],
                                      vec_s[:, 2 + layer:3 + layer], ALU.mult, ALU.add).then_inc(hn_done, 1)

                if layer == LAYERS - 1:
                    dve.tensor_tensor(b2_out[:], vec_s[:, 5:6], vec_s[:, 6:7], ALU.add).then_inc(tables_done, 1)
                    dve.wait_ge(tables_done, 4 * LAYERS + 1)
                with dve.Fori(0, SPANS) as j:
                    jj = j + SPANS * layer
                    for c, (at, size) in enumerate(HID_PARTS):
                        after(dve, gelu_done, 3 * jj + (c + 1))
                        after(dve, lin_ready, 3 * jj + (c + 1))
                        after(dve, ffn_ready, jj)
                        dve.scalar_tensor_tensor(hh[c][0:size, :], lin_ps[c % 2][0:size, :],
                                                 b1_s[0:size, layer, 0, c:c + 1], gelu_s[c % 2][0:size, :],
                                                 ALU.add, ALU.mult).then_inc(hh_done, 1)
                    after(dve, ffn_ready, jj + 1)
                    if layer < LAYERS - 1:
                        dve.scalar_tensor_tensor(xin[:, cols(j * WIDE + 1, WIDE)], ffn_ps,
                                                 vec_s[:, 4 + layer:5 + layer], x1[:, cols(j * WIDE, WIDE)],
                                                 ALU.add, ALU.add).then_inc(x2_done, 1)
                    else:
                        dve.scalar_tensor_tensor(sum_t, ffn_ps, b2_out[:], x1[:, cols(j * WIDE, WIDE)],
                                                 ALU.add, ALU.add).then_inc(x2_done, 1)
                        after(dve, tr_ready, j + 1)
                        after(dve, stored, 16 * j)
                        dve.tensor_tensor(out_s[:], tr_ps,
                                          x_raw[:].rearrange("p t d -> p (t d)")[:, cols(j * WIDE, WIDE)],
                                          ALU.add).then_inc(out_done, 1)


def kernel(**inputs):
    import concourse.bacc as bacc
    from concourse.bass_utils import run_bass_kernel_spmd

    named = {
        "x": inputs["L0_attn_x"],
        "a_wqkv_t": np.transpose(inputs["L0_attn_Wqkv"]),
        "a_wout_t": np.transpose(inputs["L0_attn_Wout"]),
        "wqkv": inputs["L0_ffn_wqkv"],
        "q_scale": inputs["L0_ffn_q_scale"],
        "k_scale": inputs["L0_ffn_k_scale"],
        "wo": inputs["L0_ffn_wo"],
        "w1": inputs["L0_ffn_w1"],
        "w2": inputs["L0_ffn_w2"],
        "vectors": pack_vectors(**{k: inputs["L0_" + k] for k in
                                   ("ffn_b1", "ffn_ln_g", "ffn_ln_b", "ffn_b2", "attn_bout")}),
        **constants(),
    }
    nc = bacc.Bacc("TRN2", target_bir_lowering=False, num_devices=1)
    arrays, args = {}, []
    for name, a in named.items():
        a = np.ascontiguousarray(a)
        arrays[f"in_{name}"] = a
        args.append(nc.dram_tensor(f"in_{name}", a.shape, mybir.dt.from_np(a.dtype), kind="ExternalInput").ap())
    out = nc.dram_tensor("out", (1, N, DIM), F32, kind="ExternalOutput").ap()
    build(nc, *args, out)
    r = run_bass_kernel_spmd(nc, [arrays], core_ids=[0])
    return r.results[0]["out"]
```

```python
from contextlib import ExitStack

import numpy as np

import concourse.bass as bass
import concourse.mybir as mybir
from concourse.alu_op_type import AluOpType as ALU

F32 = mybir.dt.float32
F32R = mybir.dt.float32r
BF16 = mybir.dt.bfloat16
ACT = mybir.ActivationFunctionType
AX = mybir.AxisListType

P = 128
N = 2048
DIM = 128
TILES = N // P
LAYERS = 2
HEADS, DH = 8, 64
HALF = DH // 2
INNER = HEADS * DH
WINDOW = 64
CHUNKS = INNER // P
QK_SCALE = 8.0
HID = int(DIM * 4 * 2 / 3)
HID_PARTS = [(0, 128), (128, 128), (256, HID - 256)]
LN_EPS = 1e-5
WIDE = 512
SPANS = N // WIDE
MASKED = -1e30

PATCH, SHIFT = 20, 2
BLOCK = PATCH * SHIFT
PATCH_BLOCKS = 13
PATCHED = PATCH_BLOCKS * BLOCK
A_HEADS, A_DH = 16, 8
A_SCALE = A_DH ** -0.5
A_STEP = 2 * BLOCK
A_STEPS = -(-PATCHED // A_STEP)
A_WIN = 112
W_PARTS = 2
W_PART = 3 * INNER // W_PARTS
QUADS = 4

LN_SHIFT = 2.0 ** 16
LN_UNSHIFT = float(np.log(2.0 ** 8))
NORM_FLOOR_SQ = 1e-24


def constants():
    half_idx = np.arange(0, DH, 2, dtype=np.float32)
    inv_freq = (1.0 / 10000.0 ** (half_idx / DH)).astype(np.float32)
    t = np.arange(N, dtype=np.float32)
    freqs = (t[:, None] * inv_freq[None, :]).astype(np.float32).astype(np.float64)
    base = (half_idx.astype(np.float64) + 0.4 * DH) / (1.4 * DH)
    scale = base[None, :] ** ((t.astype(np.float64)[:, None] - N // 2) / (WINDOW // 2))
    cos, sin = np.cos(freqs), np.sin(freqs)

    def table(parts):
        full = np.stack([np.concatenate(x, 1) for x in parts], 1).astype(np.float32)
        return np.ascontiguousarray(full.reshape(TILES, P, 2, DH).transpose(1, 0, 2, 3))

    qs, ks = scale * QK_SCALE, 1.0 / scale
    cos_t = table([(cos * qs, cos * qs), (cos * ks, cos * ks)])
    sin_t = table([(sin * qs, -sin * qs), (sin * ks, -sin * ks)])

    ident = np.eye(P, dtype=np.float32)
    i = np.arange(P)[:, None] % WINDOW
    j = np.arange(2 * WINDOW)[None, :]
    usual = np.where((j >= i) & (j <= i + WINDOW), 0.0, MASKED)
    first = np.where((j >= WINDOW) & (j <= i + WINDOW), 0.0, MASKED)
    mask = np.stack([np.tile(usual, (1, 4)), np.concatenate([first, usual] * 2, 1)], 1)
    center = ident - 1.0 / P
    mean = np.full((P, P), 1.0 / P, np.float32)
    head_of = (np.arange(P)[:, None] % 32) // A_DH == np.arange(4)[None, :]
    key_head = np.arange(4 * PATCH) // PATCH
    value_head = (np.arange(P) % 32) // A_DH
    value_mask = np.zeros((P, P), np.float32)
    value_mask[:4 * PATCH] = key_head[:, None] == value_head[None, :]
    small = np.concatenate([ident, center, mean, value_mask, head_of], 1).astype(np.float32)
    masks = np.concatenate([ident, mask.reshape(P, -1)], 1).astype(np.float32)
    return {"cos_t": cos_t, "sin_t": sin_t, "small": small, "masks": masks}


def pack_vectors(ffn_b1, ffn_ln_g, ffn_ln_b, ffn_b2, attn_bout):
    b1 = np.zeros((LAYERS, 2, 3 * P), np.float32)
    b1[:, :, :HID] = np.reshape(ffn_b1, (LAYERS, 2, HID))
    rows = [b1.reshape(12, P), ffn_ln_g, ffn_ln_b, ffn_b2, np.reshape(attn_bout, (1, P))]
    return np.concatenate([np.asarray(r) for r in rows], 0).T


def after(eng, sem, count):
    if not isinstance(count, int) or count > 0:
        eng.wait_ge(sem, count)


def over_tiles(eng, step):
    for t in range(-1, 4):
        step(t, t % 2)
    with eng.Fori(2, TILES // 2 - 1) as i:
        step(i * 2, 0)
        step(i * 2 + 1, 1)
    for t in range(TILES - 2, TILES + 2):
        step(t, t % 2)


def is_at(t, value):
    return isinstance(t, int) and t == value


def norm_span(t):
    first = TILES - 2
    return t - first if isinstance(t, int) and first <= t < first + SPANS - 1 else None


def there(t, count=TILES):
    return not isinstance(t, int) or 0 <= t < count


def over_patches(eng, step, in_front=lambda t: None):
    for t in range(-1, 2):
        in_front(t)
        step(t, t % 2)
    with eng.Fori(1, A_STEPS // 2) as i:
        step(i * 2, 0)
        step(i * 2 + 1, 1)
    for t in range(2 * (A_STEPS // 2), A_STEPS + 1):
        in_front(t)
        step(t, t % 2)


def early_tile(layer, j):
    return j - (SPANS - 2) if layer < LAYERS - 1 and isinstance(j, int) and j >= SPANS - 2 else None


def matmul3(pe, out, stationary, moving, start=True, stop=True):
    (s_hi, s_lo), (m_hi, m_lo) = stationary, moving
    pe.matmul(out, s_hi, m_hi, start=start, stop=False)
    pe.matmul(out, s_hi, m_lo, start=False, stop=False)
    return pe.matmul(out, s_lo, m_hi, start=False, stop=stop)


def cols(start, size):
    return slice(start, start + size) if isinstance(start, int) else bass.ds(start, size)


def build(nc, x, a_wqkv_t, a_wout_t, wqkv, q_scale, k_scale, wo, w1, w2, vectors_d,
          cos_d, sin_d, small_d, masks_d, out):
    ctx = ExitStack()
    with ctx:
        def sb(name, shape, dt=F32):
            return ctx.enter_context(nc.sbuf_tensor(name, shape, dt))

        def sem(name):
            return ctx.enter_context(nc.semaphore(name))

        small = sb("small", [P, 4 * P + 4])
        ident, center_w, mean_w = small[:, 0:P], small[:, P:2 * P], small[:, 2 * P:3 * P]
        value_mask, head_mask = small[:, 3 * P:4 * P], small[:, 4 * P:4 * P + 4]
        masks = sb("masks", [P, P + 2 * WIDE], BF16)
        ident_bf, usual_mask, first_mask = masks[:, 0:P], masks[:, P:P + WIDE], masks[:, P + WIDE:]
        cos_raw = sb("cos_raw", [P, TILES, 2, DH])
        sin_raw = sb("sin_raw", [P, TILES, 2, DH])
        cos_w = sb("cos_w", [P, TILES, 2, DH])
        sin_w = sb("sin_w", [P, TILES, 2, DH])
        qk_scale = sb("qk_scale", [P, LAYERS, 2, DH])
        a_wqkv_s = sb("a_wqkv_s", [P, 3 * DIM])
        a_wout_s = sb("a_wout_s", [P, DIM])
        wqkv_hi = sb("wqkv_hi", [P, LAYERS, 3 * INNER], F32R)
        wqkv_lo = sb("wqkv_lo", [P, LAYERS, 3 * INNER], F32R)
        wo_s = sb("wo_s", [P, LAYERS, CHUNKS, DIM])
        w1_hi = sb("w1_hi", [P, LAYERS, 2 * HID], F32R)
        w1_lo = sb("w1_lo", [P, LAYERS, 2 * HID], F32R)
        w_raw = sb("w_raw", [P, 3 * INNER])
        w2_s = sb("w2_s", [P, LAYERS, 3, DIM])
        vectors = sb("vectors", [P, 19])
        b1_s = vectors[:, 0:12].rearrange("p (l a c) -> p l a c", l=LAYERS, a=2)
        vec_s = vectors[:, 12:19]
        b2_out = sb("b2_out", [P, 1])
        eps_s = sb("eps_s", [P, 2])

        x_raw = sb("x_raw", [P, TILES, DIM])
        xn_tok = sb("xn_tok", [P, TILES, DIM])
        stats = sb("stats", [P, TILES, 6])
        mv = sb("mv", [P, TILES, 2])
        ln0 = sb("ln0", [P, TILES])
        rstd0 = sb("rstd0", [P, TILES])
        xin = sb("xin", [P, 1 + N])
        x1 = sb("x1", [P, N])
        masks_f = x1[:, 0:P + 2 * WIDE]
        x1_shift = sb("x1_shift", [P, 1 + N])
        x_patch = sb("x_patch", [P, N])
        hn_hi = sb("hn_hi", [P, N], F32R)
        hn_lo = sb("hn_lo", [P, N], F32R)
        hn = xn_tok[:].rearrange("p t d -> p (t d)")

        wqkv_raw = [x1_shift[:, 1:1 + 3 * INNER], w_raw[:]]
        w1_raw = hn[:, 0:2 * LAYERS * HID].rearrange("p (l n) -> p l n", l=LAYERS)

        stage = [sb(f"stage{i}", [P, P]) for i in range(2)]
        stage_hi = [sb(f"stage_hi{i}", [P, P], F32R) for i in range(2)]
        stage_lo = [sb(f"stage_lo{i}", [P, P], F32R) for i in range(2)]
        sq = sb("sq", [P, 2 * INNER])
        ss = sb("ss", [P, 2 * HEADS])
        ssc = sb("ssc", [P, 2 * HEADS])
        lnss = sb("lnss", [P, 2 * HEADS])
        rnorm = sb("rnorm", [P, 2 * HEADS])
        cos_now = sb("cos_now", [P, 2, DH])
        qkn = sb("qkn", [P, 2 * INNER])
        rot1 = sb("rot1", [P, 2 * INNER])
        rot2 = sb("rot2", [P, 2 * INNER])
        q_diag = sb("q_diag", [P, CHUNKS, 2, P])
        k_t = [sb(f"k_t{i}", [P, CHUNKS, WINDOW + P]) for i in range(2)]
        v_tok = [sb(f"v_tok{i}", [P, INNER]) for i in range(2)]
        v_off = [sb(f"v_off{i}", [P, INNER]) for i in range(2)]
        neg_max = sb("neg_max", [P, 8])
        row_sum = sb("row_sum", [P, 8])
        row_inv = sb("row_inv", [P, 8])
        probs = sb("probs", [P, 8, P])
        probs_n = sb("probs_n", [P, 8, P])
        probs_t = [sb("probs_t", [P, 8, P]), w_raw[:, 0:8 * P].rearrange("p (a k) -> p a k", a=8)]
        o_t = sb("o_t", [P, INNER])

        def halves(tensor):
            return [tensor[:, 0:WIDE], tensor[:, WIDE:2 * WIDE]]

        (ln_sq, ln_log), ln_rstd = halves(sq), halves(qkn)
        gelu_s = v_off
        hh = probs[:].rearrange("p a k -> p (a k)").rearrange("p (a k) -> p a k", k=WIDE)
        hh = [hh[:, 0, :], hh[:, 1, :], probs_n[:, 0:4, :].rearrange("p a k -> p (a k)")]
        sum_t = probs_n[:, 4:8, :].rearrange("p a k -> p (a k)")
        out_s = o_t

        flat = {name: b[:].rearrange("p a k -> p (a k)")
                for name, b in (("probs", probs), ("probs_n", probs_n), ("probs_t", probs_t[0]))}
        a_v = [b[0:4 * PATCH, 0:4 * DIM].rearrange("p (j d) -> p j d", j=4) for b in (flat["probs"], o_t)]
        a_pt = flat["probs"][0:4 * PATCH, WIDE:2 * WIDE]
        a_k = flat["probs_n"][:, 0:4 * A_WIN].rearrange("p (h c) -> p h c", h=4)
        a_x = flat["probs_n"][:, WIDE:WIDE + A_WIN]
        a_q = flat["probs_n"][:, WIDE + P:WIDE + P + A_WIN]
        a_rep = flat["probs_t"][:, 0:16 * PATCH].rearrange("p (j r i) -> p j r i", j=4, r=4)
        a_p = flat["probs_t"][:, 16 * PATCH:32 * PATCH].rearrange("p (h k) -> p h k", k=PATCH)
        a_pn = flat["probs_t"][:, 32 * PATCH:48 * PATCH].rearrange("p (h k) -> p h k", k=PATCH)
        a_dif = sb("a_dif", [P, A_HEADS, PATCH])
        a_max = sb("a_max", [P, A_HEADS])
        a_sum = sb("a_sum", [P, A_HEADS])
        a_inv = sb("a_inv", [P, A_HEADS])
        a_o = sb("a_o", [P, DIM])

        ps = ctx.enter_context(nc.psum_tensor("ps", [P, 8 * WIDE], F32))

        def bank(b, n=1):
            return ps[:, b * WIDE:(b + n) * WIDE]

        qk_ps = bank(0, 2)
        v_ps = bank(2)
        s_ps = [bank(3), bank(4)]
        ot_ps = bank(5)
        y_ps = ot_ps
        turn_ps = bank(6, 2)
        cen_ps = [bank(0), bank(2)]
        var_ps = bank(1)
        gate_ps = [bank(6), bank(7)]
        lin_ps = [bank(3), bank(4)]
        ffn_ps = bank(5)
        tr_ps = bank(0)
        a_s = bank(0, 4).rearrange("p (g c) -> p g c", g=4)[:, :, 0:4 * PATCH]
        a_q_ps = bank(4)[:, 0:A_WIN]
        a_k_ps = bank(4)[:, P:P + A_WIN]
        a_vr = bank(6)
        a_tp = bank(5)
        a_op = bank(7)
        t0_ps = [bank(7), bank(7), bank(5), bank(7)]

        x_in = [sem(f"x_in{g}") for g in range(SPANS)]
        masks_in = sem("masks_in")
        const_in = sem("const_in")
        aw_in = sem("aw_in")
        tab_in = sem("tab_in")
        wqkv_in = [sem(f"wqkv_in{layer}") for layer in range(LAYERS)]
        w_in = sem("w_in")
        w1_in = sem("w1_in")
        w1_split = sem("w1_split")
        wqkv_rounded = sem("wqkv_rounded")
        wqkv_split = sem("wqkv_split")
        staged_raw = sem("staged_raw")
        staged_hi = sem("staged_hi")
        hn_split = sem("hn_split")
        fw_in = sem("fw_in")
        zeroed = sem("zeroed")
        stat_done = sem("stat_done")
        mv_done = sem("mv_done")
        ln0_done = sem("ln0_done")
        rstd0_done = sem("rstd0_done")
        xn_done = sem("xn_done")
        xn_tr = sem("xn_tr")
        xin0_done = sem("xin0_done")
        a_staged = sem("a_staged")
        a_qk_done = sem("a_qk_done")
        a_vr_done = sem("a_vr_done")
        a_q_done = sem("a_q_done")
        a_k_done = sem("a_k_done")
        a_v_done = sem("a_v_done")
        a_s_done = sem("a_s_done")
        a_max_done = sem("a_max_done")
        a_dif_done = sem("a_dif_done")
        a_p_done = sem("a_p_done")
        a_sum_done = sem("a_sum_done")
        a_inv_done = sem("a_inv_done")
        a_pn_done = sem("a_pn_done")
        a_tp_done = sem("a_tp_done")
        a_pt_done = sem("a_pt_done")
        a_op_done = sem("a_op_done")
        a_o_done = sem("a_o_done")
        a_ot_done = sem("a_ot_done")
        a_out_done = sem("a_out_done")
        patch_rest_done = sem("patch_rest_done")
        tables_done = sem("tables_done")
        b2_done = sem("b2_done")
        masks_done = sem("masks_done")
        staged = sem("staged")
        qk_ready = sem("qk_ready")
        v_ready = sem("v_ready")
        sq_done = sem("sq_done")
        ss_done = sem("ss_done")
        lnss_done = sem("lnss_done")
        rnorm_done = sem("rnorm_done")
        qkn_done = sem("qkn_done")
        rot_done = sem("rot_done")
        rot_summed = sem("rot_summed")
        cos_taken = sem("cos_taken")
        qkt_ready = sem("qkt_ready")
        qkt_evac = sem("qkt_evac")
        v_evac = sem("v_evac")
        v_off_in = sem("v_off_in")
        s_ready = sem("s_ready")
        max_done = sem("max_done")
        probs_done = sem("probs_done")
        inv_done = sem("inv_done")
        probs_n_done = sem("probs_n_done")
        pt_ready = sem("pt_ready")
        pt_evac = [sem(f"pt_evac{g}") for g in range(2)]
        ot_ready = sem("ot_ready")
        ot_evac = sem("ot_evac")
        y_ready = sem("y_ready")
        x1_done = sem("x1_done")
        x1_shifted = sem("x1_shifted")
        cen_ready = sem("cen_ready")
        ln_sq_done = sem("ln_sq_done")
        var_ready = sem("var_ready")
        ln_log_done = sem("ln_log_done")
        ln_rstd_done = sem("ln_rstd_done")
        hn_scaled = sem("hn_scaled")
        hn_done = sem("hn_done")
        gate_ready = sem("gate_ready")
        lin_ready = sem("lin_ready")
        gelu_done = sem("gelu_done")
        hh_done = sem("hh_done")
        ffn_ready = sem("ffn_ready")
        x2_done = sem("x2_done")
        tr_ready = sem("tr_ready")
        out_done = sem("out_done")
        stored = sem("stored")

        block = ctx.enter_context(nc.Block())

        @block.sync
        def _(sp):
            for g in range(SPANS):
                sp.dma_start(x_raw[:, 4 * g:4 * g + 4, :],
                             x[0, g * WIDE:(g + 1) * WIDE, :].rearrange("(t p) d -> p t d", p=P)).then_inc(x_in[g], 16)
            sp.dma_start(masks_f, masks_d).then_inc(masks_in, 16)
            for layer in range(LAYERS):
                sp.dma_start(wqkv_raw[layer], wqkv[layer]).then_inc(wqkv_in[layer], 16)
            sp.dma_start(cos_raw[:], cos_d).then_inc(tab_in, 16)
            sp.dma_start(sin_raw[:], sin_d).then_inc(tab_in, 16)
            for part, scale in enumerate((q_scale, k_scale)):
                sp.dma_start(qk_scale[:, :, part, :], scale.partition_broadcast(P)).then_inc(tab_in, 16)
            sp.dma_start(wo_s[:], wo.rearrange("l (c p) n -> p l c n", p=P)).then_inc(w_in, 16)
            sp.dma_start(a_wout_s[:], a_wout_t).then_inc(fw_in, 16)
            for c, (at, size) in enumerate(HID_PARTS):
                sp.dma_start(w2_s[0:size, :, c, :],
                             w2[:, at:at + size, :].rearrange("l p n -> p l n")).then_inc(fw_in, 16)
            sp.dma_start(vectors[:], vectors_d).then_inc(fw_in, 16)
            sp.wait_ge(xn_tr, SPANS)
            sp.dma_start(w1_raw, w1.rearrange("l p n -> p l n")).then_inc(w1_in, 16)

            def shift_values(n, parity):
                after(sp, v_evac, n + 1)
                sp.dma_start(v_off[parity][0:WINDOW, :], v_tok[1 - parity][WINDOW:P, :]).then_inc(v_off_in, 16)
                sp.dma_start(v_off[parity][WINDOW:P, :], v_tok[parity][0:WINDOW, :]).then_inc(v_off_in, 16)

            sp.wait_ge(zeroed, 7)
            for layer in range(LAYERS):
                def step(t, parity):
                    if there(t):
                        shift_values(t + layer * TILES, parity)

                over_tiles(sp, step)
            for j in range(SPANS):
                sp.wait_ge(out_done, j + 1)
                sp.dma_start(out[0, cols(j * WIDE, WIDE), :].rearrange("(q p) d -> p q d", p=P),
                             out_s[:].rearrange("p (q d) -> p q d", q=4)).then_inc(stored, 16)
            sp.wait_ge(stored, 16 * SPANS)

        @block.gpsimd
        def _(pool):
            pool.memset(xin[:, 0:1], 0.0).then_inc(zeroed, 1)
            pool.memset(x1_shift[:, 0:1], 0.0).then_inc(zeroed, 1)
            pool.memset(v_tok[1][:], 0.0).then_inc(zeroed, 1)
            pool.memset(k_t[0][:], 0.0).then_inc(zeroed, 1)
            pool.memset(eps_s[:, 0:1], LN_EPS).then_inc(zeroed, 1)
            pool.memset(eps_s[:, 1:2], LN_UNSHIFT).then_inc(zeroed, 1)
            pool.memset(q_diag[:], 0.0).then_inc(zeroed, 1)

            pool.wait_ge(masks_in, 16)
            pool.tensor_copy(masks[:], masks_f).then_inc(masks_done, 1)

            def scale_tables(layer):
                for raw, table in ((cos_raw, cos_w), (sin_raw, sin_w)):
                    for part in range(2):
                        pool.tensor_tensor(table[:, :, part, :], raw[:, :, part, :],
                                           qk_scale[:, layer, part, :].unsqueeze(1).broadcast_to([P, TILES, DH]),
                                           ALU.mult).then_inc(tables_done, 1)

            pool.wait_ge(tab_in, 64)
            scale_tables(0)

            def split_wqkv(layer):
                pool.wait_ge(wqkv_rounded, W_PARTS * (layer + 1))
                pool.tensor_tensor(wqkv_lo[:, layer, :], wqkv_raw[layer], wqkv_hi[:, layer, :],
                                   ALU.subtract).then_inc(wqkv_split, 1)

            split_wqkv(0)
            pool.wait_ge(wqkv_split, 1)
            pool.wait_ge(tables_done, 4)
            pool.wait_ge(masks_done, 1)
            pool.wait_ge(xin0_done, SPANS)

            def make_stage(n, t, parity):
                after(pool, probs_n_done, 2 * n - 4)
                after(pool, staged, n - 1)
                pool.tensor_copy(stage[parity][0:64, :], xin[0:64, cols(t * P + 1, P)]).then_inc(staged_raw, 1)
                pool.tensor_copy(stage[parity][64:P, :], xin[64:P, cols(t * P, P)]).then_inc(staged_raw, 1)

            def rotate_cos(n, t, ended):
                after(pool, staged_raw, ended)
                after(pool, x1_shifted, 2 * n - 6)
                pool.tensor_copy(cos_now[:], cos_w[:, cols(t, 1), :, :].rearrange("p a b d -> p (a b) d")
                                 ).then_inc(cos_taken, 1)
                after(pool, cos_taken, n - layer)
                after(pool, qkn_done, n + 1)
                after(pool, rot_summed, 2 * n)
                pool.tensor_tensor(rot1[:].rearrange("p (a h d) -> p a h d", a=2, d=DH),
                                   qkn[:].rearrange("p (a h d) -> p a h d", a=2, d=DH),
                                   cos_now[:].unsqueeze(2).broadcast_to([P, 2, HEADS, DH]),
                                   ALU.mult).then_inc(rot_done, 1)

            def normalize(n, g, ended):
                after(pool, staged_raw, ended)
                after(pool, x1_shifted, 2 * n - 4)
                after(pool, inv_done, 2 * n + (g + 1))
                after(pool, pt_ready, 2 * n + (g - 1))
                pool.tensor_tensor(probs_n[:, 4 * g:4 * g + 4, :], probs[:, 4 * g:4 * g + 4, :],
                                   row_inv[:, 4 * g:4 * g + 4].unsqueeze(2).broadcast_to([P, 4, P]),
                                   ALU.mult).then_inc(probs_n_done, 1)

            def shift_x1(n, t, ended):
                after(pool, probs_n_done, ended)
                after(pool, x1_done, n + 1)
                pool.tensor_copy(x1_shift[0:64, cols(t * P, P)], x1[0:64, cols(t * P, P)]).then_inc(x1_shifted, 1)
                pool.tensor_copy(x1_shift[64:P, cols(t * P + 1, P)], x1[64:P, cols(t * P, P)]).then_inc(x1_shifted, 1)

            for layer in range(LAYERS):
                n0 = layer * TILES

                def step(t, parity):
                    n = t + n0
                    if layer > 0 and is_at(t, 0):
                        pool.wait_ge(x2_done, SPANS * layer)
                    if there(t + 2) and not is_at(t, -1):
                        make_stage(n + 2, t + 2, parity)
                    if there(t + 1) and not is_at(t, -1):
                        rotate_cos(n + 1, t + 1, 2 * n + 6 if there(t + 2) else 2 * (n0 + TILES))
                    if there(t):
                        for g in range(2):
                            normalize(n, g, 2 * n + 6 if there(t + 2) else 2 * (n0 + TILES))
                    if there(t - 2):
                        shift_x1(n - 2, t - 2, 2 * n + 2 if there(t) else 2 * (n0 + TILES))

                if layer > 0:
                    pool.wait_ge(tables_done, 4 * (layer + 1))
                    pool.wait_ge(x2_done, SPANS * (layer - 1) + 1)
                for t in range(2):
                    make_stage(n0 + t, t, t)
                if layer == 0:
                    pool.wait_ge(staged_raw, 4)
                    pool.wait_ge(w1_in, 16)
                    for other in range(LAYERS):
                        pool.tensor_copy(w1_hi[:, other, :], w1_raw[:, other, :]).then_inc(w1_split, 1)
                        pool.wait_ge(w1_split, 2 * other + 1)
                        pool.tensor_tensor(w1_lo[:, other, :], w1_raw[:, other, :], w1_hi[:, other, :],
                                           ALU.subtract).then_inc(w1_split, 1)
                    split_wqkv(1)
                    pool.tensor_copy(x_patch[:, PATCHED:N], xin[:, 1 + PATCHED:1 + N]).then_inc(patch_rest_done, 1)
                    pool.wait_ge(w1_split, 2 * LAYERS)
                    pool.wait_ge(wqkv_split, LAYERS)
                    pool.wait_ge(patch_rest_done, 1)
                over_tiles(pool, step)
                if layer < LAYERS - 1:
                    pool.wait_ge(x1_shifted, 2 * (n0 + TILES))
                    pool.wait_ge(rot_done, 3 * TILES * (layer + 1))
                    scale_tables(layer + 1)

        @block.tensor
        def _(pe):
            def turn_input(g):
                pe.wait_ge(xn_done, 4 * g + 4)
                if g != 2:
                    after(pe, xin0_done, min(g, 2))
                for q in range(4):
                    mm = pe.transpose(t0_ps[g][:, q * P:(q + 1) * P], xn_tok[:, 4 * g + q, :], ident)
                mm.then_inc(xn_tr, 1)

            def project_qk(layer, n, parity):
                after(pe, staged, n + 1)
                after(pe, qkn_done, n)
                for part in range(2):
                    span = slice(part * INNER, (part + 1) * INNER)
                    mm = matmul3(pe, qk_ps[:, span], (stage_hi[parity][:], stage_lo[parity][:]),
                                 (wqkv_hi[:, layer, span], wqkv_lo[:, layer, span]))
                mm.then_inc(qk_ready, 1)

            def turn_patch_probs(t):
                after(pe, a_pn_done, t + 1)
                for g in range(QUADS):
                    mm = pe.transpose(a_tp[0:4 * PATCH, g * P:(g + 1) * P],
                                      a_pn[:, 4 * g:4 * g + 4, :].rearrange("p h k -> p (h k)"), ident)
                mm.then_inc(a_tp_done, 1)

            def patch_scores(t):
                for j in range(4):
                    at = BLOCK * (j // 2) + j % 2
                    for g in range(QUADS):
                        mm = pe.matmul(a_s[32 * j:32 * j + 32, g, :],
                                       a_q[32 * g:32 * g + 32, at:at + 63:SHIFT],
                                       a_k[32 * g:32 * g + 32, :, at:at + BLOCK - 1:SHIFT],
                                       start=True, stop=True)
                mm.then_inc(a_s_done, 1)

            def weigh_patch_values(t, parity):
                after(pe, a_pt_done, t + 1)
                after(pe, a_v_done, t + 1)
                after(pe, a_out_done, t)
                if is_at(t, 0):
                    pe.wait_ge(xin0_done, SPANS)
                for j in range(4):
                    for g in range(QUADS):
                        mm = pe.matmul(a_op[32 * j:32 * j + 32, 32 * g:32 * g + 32],
                                       a_pt[:, g * P + 32 * j:g * P + 32 * j + 32],
                                       a_v[parity][:, j, 32 * g:32 * g + 32], start=True, stop=True)
                mm.then_inc(a_op_done, 1)

            def project_patch_qk(t):
                after(pe, a_staged, 3 * t + 3)
                after(pe, a_k_done, t)
                pe.matmul(a_q_ps, a_wqkv_s[:, 0:DIM], a_x, start=True, stop=True)
                pe.matmul(a_k_ps, a_wqkv_s[:, DIM:2 * DIM], a_x,
                          start=True, stop=True).then_inc(a_qk_done, 1)

            def project_patch_values(t):
                after(pe, a_v_done, t)
                for j in range(4):
                    mm = pe.matmul(a_vr[0:4 * PATCH, j * DIM:(j + 1) * DIM],
                                   a_rep[:, j, :, :].rearrange("p r i -> p (r i)"),
                                   a_wqkv_s[:, 2 * DIM:3 * DIM], start=True, stop=True)
                mm.then_inc(a_vr_done, 1)

            def turn_patch_out(t):
                after(pe, a_o_done, t + 1)
                pe.transpose(a_op[:, P:2 * P], a_o[:], ident).then_inc(a_ot_done, 1)

            def patch_step(t, parity):
                if there(t, A_STEPS):
                    project_patch_values(t)
                if there(t - 2, A_STEPS):
                    turn_patch_out(t - 2)
                if is_at(t, 1):
                    pe.wait_ge(xin0_done, 3)
                if there(t, A_STEPS):
                    after(pe, a_q_done, t + 1)
                    after(pe, a_k_done, t + 1)
                    after(pe, a_dif_done, t)
                if there(t - 1, A_STEPS):
                    turn_patch_probs(t - 1)
                if there(t, A_STEPS):
                    patch_scores(t)
                if there(t + 1, A_STEPS):
                    project_patch_qk(t + 1)
                if there(t - 1, A_STEPS):
                    weigh_patch_values(t - 1, 1 - parity)

            def in_front(t):
                if t == -1:
                    pe.wait_ge(const_in, 16)
                    turn_input(0)
                    pe.wait_ge(aw_in, 16)
                if t == 0:
                    turn_input(1)
                    turn_input(2)
                if t == 1:
                    turn_input(3)
                if t == A_STEPS:
                    pe.wait_ge(wqkv_split, 1)
                    pe.wait_ge(a_dif_done, A_STEPS)
                    project_qk(0, 0, 0)

            over_patches(pe, patch_step, in_front)
            turn_patch_out(A_STEPS - 1)
            project_qk(0, 1, 1)
            pe.wait_ge(a_out_done, A_STEPS)

            pe.wait_ge(masks_done, 1)
            pe.wait_ge(w_in, 16)
            for layer in range(LAYERS):
                def project_v(n, parity):
                    after(pe, v_evac, n)
                    span = slice(2 * INNER, 3 * INNER)
                    matmul3(pe, v_ps, (stage_hi[parity][:], stage_lo[parity][:]),
                            (wqkv_hi[:, layer, span], wqkv_lo[:, layer, span])).then_inc(v_ready, 1)

                def turn(n, part):
                    after(pe, qkt_evac, 4 * n)
                    after(pe, rot_summed, 2 * n + (part + 1))
                    for c in range(CHUNKS):
                        at = part * INNER + c * P
                        mm = pe.transpose(turn_ps[:, at:at + P], rot2[:, at:at + P], ident)
                    mm.then_inc(qkt_ready, 1)

                def scores(n, parity, g, mask):
                    after(pe, qkt_evac, 4 * n + 3)
                    after(pe, pt_evac[g], n)
                    pe.matmul(s_ps[g], ident_bf, mask, start=True, stop=False, skip_group_check=True)
                    for cw in range(4):
                        c, w = 2 * g + cw // 2, cw % 2
                        mm = pe.matmul(s_ps[g][:, cw * P:(cw + 1) * P], q_diag[:, c, w, :],
                                       k_t[parity][:, c, w * WINDOW:w * WINDOW + P],
                                       start=False, stop=True, skip_group_check=True)
                    mm.then_inc(s_ready, 1)

                def turn_probs(n, g):
                    after(pe, probs_n_done, 2 * n + (g + 1))
                    for cw in range(4):
                        mm = pe.transpose(s_ps[g][:, cw * P:(cw + 1) * P], probs_n[:, 4 * g + cw, :], ident)
                    mm.then_inc(pt_ready, 1)

                def weigh_values(n, parity):
                    after(pe, pt_evac[0], n + 1)
                    after(pe, pt_evac[1], n + 1)
                    after(pe, v_off_in, 32 * n + 32)
                    after(pe, x1_done, n)
                    for c in range(CHUNKS):
                        for w in range(2):
                            v = (v_off if w == 0 else v_tok)[parity]
                            for h in range(2):
                                head = (2 * c + h) * DH
                                mm = pe.matmul(ot_ps[64 * h:64 * h + 64, c * P + w * WINDOW:c * P + (w + 1) * WINDOW],
                                               v[:, head:head + DH],
                                               probs_t[parity][:, 2 * c + w, h * WINDOW:(h + 1) * WINDOW],
                                               start=True, stop=True)
                    mm.then_inc(ot_ready, 1)

                def project_out(n):
                    after(pe, ot_evac, n + 1)
                    for c in range(CHUNKS):
                        mm = pe.matmul(y_ps[:, 0:P], wo_s[:, layer, c, :], o_t[:, c * P:(c + 1) * P],
                                       start=(c == 0), stop=(c == CHUNKS - 1))
                    mm.then_inc(y_ready, 1)

                def centered(j):
                    jj = SPANS * layer + j
                    last_tile = TILES * layer + 4 * j + 3
                    after(pe, x1_shifted, 2 * last_tile + 2)
                    after(pe, qkn_done, TILES * (layer + 1))
                    if j > 0:
                        after(pe, v_evac, TILES * (layer + 1))
                    after(pe, hn_scaled, jj - 1)
                    pe.matmul(cen_ps[j % 2], center_w, x1_shift[:, j * WIDE:(j + 1) * WIDE],
                              start=True, stop=True).then_inc(cen_ready, 1)

                def variance(j):
                    jj = SPANS * layer + j
                    after(pe, ln_sq_done, jj + 1)
                    after(pe, ln_log_done, jj)
                    pe.matmul(var_ps, mean_w, ln_sq, start=True, stop=True).then_inc(var_ready, 1)

                def step(t, parity):
                    n = t + layer * TILES
                    j = norm_span(t)
                    if there(t):
                        mask = first_mask if isinstance(t, int) and t == 0 else usual_mask
                        scores(n, parity, 0, mask)
                        scores(n, parity, 1, mask)
                    if there(t - 2):
                        project_out(n - 2)
                    if j is not None:
                        centered(j)
                    if there(t + 2) and not is_at(t, -1):
                        project_qk(layer, n + 2, parity)
                    if there(t - 1):
                        weigh_values(n - 1, 1 - parity)
                    if there(t + 1):
                        turn(n + 1, 0)
                    if there(t):
                        turn_probs(n, 0)
                    if there(t + 1):
                        turn(n + 1, 1)
                    if there(t):
                        turn_probs(n, 1)
                    if j is not None:
                        variance(j)
                    if there(t + 1):
                        project_v(n + 1, 1 - parity)

                over_tiles(pe, step)

                if layer == 0:
                    pe.wait_ge(fw_in, 16 * 5)
                if layer == LAYERS - 1:
                    pe.wait_ge(patch_rest_done, 1)

                def turn_out(j):
                    after(pe, x2_done, SPANS * layer + j + 1)
                    after(pe, out_done, j)
                    for q in range(4):
                        mm = pe.transpose(tr_ps[:, q * P:(q + 1) * P], sum_t[:, q * P:(q + 1) * P], ident)
                    mm.then_inc(tr_ready, 1)

                def span(j):
                    jj = j + SPANS * layer
                    early = early_tile(layer, j)
                    after(pe, hn_split, 2 * jj + 2)
                    for c, (at, size) in enumerate(HID_PARTS):
                        after(pe, hh_done, 3 * jj if c < 2 else 3 * jj + 1)
                        gate, lin = slice(HID + at, HID + at + size), slice(at, at + size)
                        h = hn_hi[:, cols(j * WIDE, WIDE)], hn_lo[:, cols(j * WIDE, WIDE)]
                        matmul3(pe, gate_ps[c % 2][0:size, :],
                                (w1_hi[:, layer, gate], w1_lo[:, layer, gate]), h).then_inc(gate_ready, 1)
                        if is_at(j, 1) and c == 1:
                            variance(SPANS - 1)
                        matmul3(pe, lin_ps[c % 2][0:size, :],
                                (w1_hi[:, layer, lin], w1_lo[:, layer, lin]), h).then_inc(lin_ready, 1)
                        if is_at(j, 1) and c == 0:
                            centered(SPANS - 1)
                        if early is not None and c == 1:
                            after(pe, wqkv_split, layer + 2)
                            after(pe, ln_log_done, SPANS * (layer + 1))
                            after(pe, hn_scaled, SPANS * (layer + 1))
                            project_qk(layer + 1, TILES * (layer + 1) + early, early)
                    if layer == LAYERS - 1 and there(j - 1, SPANS):
                        turn_out(j - 1)
                    after(pe, x2_done, jj)
                    if layer == LAYERS - 1:
                        pe.matmul(ffn_ps, a_wout_s[:], x_patch[:, cols(j * WIDE, WIDE)], start=True, stop=False)
                    for c, (at, size) in enumerate(HID_PARTS):
                        after(pe, hh_done, 3 * jj + (c + 1))
                        mm = pe.matmul(ffn_ps, w2_s[0:size, layer, c, :], hh[c][0:size, :],
                                       start=(c == 0 and layer < LAYERS - 1), stop=(c == 2))
                    mm.then_inc(ffn_ready, 1)

                for j in range(SPANS):
                    span(j)
                if layer == LAYERS - 1:
                    turn_out(SPANS - 1)

        @block.scalar
        def _(act):
            act.dma_start(small[:], small_d).then_inc(const_in, 16)
            act.dma_start(a_wqkv_s[:], a_wqkv_t).then_inc(aw_in, 16)
            act.preload_act_table_set("natural_log_exp_and_others")
            act.wait_ge(zeroed, 7)

            def input_rstd(g):
                act.wait_ge(mv_done, 4 * g + 4)
                act.activation(ln0[:, 4 * g:4 * g + 4], mv[:, 4 * g:4 * g + 4, 1], ACT.Ln,
                               bias=eps_s[:, 0:1]).then_inc(ln0_done, 1)
                act.wait_ge(ln0_done, g + 1)
                act.activation(rstd0[:, 4 * g:4 * g + 4], ln0[:, 4 * g:4 * g + 4], ACT.Exp,
                               scale=-0.5).then_inc(rstd0_done, 1)

            def take_input(g):
                act.wait_ge(xn_tr, g + 1)
                act.copy(xin[:, 1 + g * WIDE:1 + (g + 1) * WIDE], t0_ps[g]).then_inc(xin0_done, 1)

            def round_part(layer, at):
                act.copy(wqkv_hi[:, layer, cols(at, W_PART)],
                         wqkv_raw[layer][:, cols(at, W_PART)]).then_inc(wqkv_rounded, 1)

            def patch_step(t, parity):
                if there(t - 1, A_STEPS):
                    after(act, a_tp_done, t)
                    after(act, a_op_done, t - 1)
                    act.copy(a_pt, a_tp[0:4 * PATCH, :]).then_inc(a_pt_done, 1)
                if there(t, A_STEPS):
                    after(act, a_dif_done, t + 1)
                    act.activation(a_p, a_dif[:], ACT.Exp).then_inc(a_p_done, 1)
                if there(t + 1, A_STEPS):
                    after(act, a_qk_done, t + 2)
                    after(act, a_s_done, t + 1)
                    act.mul(a_q, a_q_ps, A_SCALE).then_inc(a_q_done, 1)
                    for h in range(4):
                        k = act.mul(a_k[:, h, :], a_k_ps, head_mask[:, h:h + 1])
                    k.then_inc(a_k_done, 1)
                if is_at(t, 0) or is_at(t, 1):
                    if t == 0:
                        act.wait_ge(wqkv_in[0], 16)
                    round_part(0, t * W_PART)
                if not isinstance(t, int) and parity == 0:
                    round_part(1, t * (W_PART // 2) - W_PART)

            def norms(n):
                after(act, qk_ready, n + 1)
                act.activation(sq[:], qk_ps, ACT.Square).then_inc(sq_done, 1)

            def inverse_norms(n):
                after(act, ss_done, 2 * n + 2)
                act.activation(lnss[:], ssc[:], ACT.Ln, scale=LN_SHIFT).then_inc(lnss_done, 1)
                after(act, lnss_done, n + 1)
                act.activation(rnorm[:], lnss[:], ACT.Exp, scale=-0.5, bias=eps_s[:, 1:2]).then_inc(rnorm_done, 1)

            def in_front(t):
                if t == -1:
                    act.wait_ge(const_in, 16)
                    input_rstd(0)
                    take_input(0)
                    input_rstd(1)
                if t == 0:
                    input_rstd(2)
                    input_rstd(3)
                    take_input(1)
                    take_input(2)
                if t == 1:
                    take_input(3)
                    act.wait_ge(wqkv_in[1], 16)
                if t == A_STEPS:
                    norms(0)

            over_patches(act, patch_step, in_front)
            inverse_norms(0)
            norms(1)

            for layer in range(LAYERS):
                def take_v(n, parity):
                    after(act, v_ready, n + 1)
                    after(act, v_off_in, 32 * n)
                    act.copy(v_tok[parity][:], v_ps).then_inc(v_evac, 1)

                def take_q(n):
                    after(act, qkt_ready, 2 * n + 1)
                    for h in range(2):
                        rows = slice(64 * h, 64 * h + 64)
                        act.copy(q_diag[rows, :, :, 64 * h:64 * h + 64].rearrange("p c w q -> p (c w) q"),
                                 turn_ps[rows, 0:INNER].rearrange("p (cw q) -> p cw q", q=WINDOW)
                                 ).then_inc(qkt_evac, 1)

                k_new = turn_ps[:, INNER:].rearrange("p (c k) -> p c k", c=CHUNKS)

                def take_k(n, parity):
                    after(act, qkt_ready, 2 * n + 2)
                    act.copy(k_t[parity][:, :, WINDOW:], k_new).then_inc(qkt_evac, 1)

                def pass_k_on(parity, last_tile):
                    if last_tile:
                        act.memzero(k_t[1 - parity][:, :, 0:WINDOW]).then_inc(qkt_evac, 1)
                    else:
                        act.copy(k_t[1 - parity][:, :, 0:WINDOW], k_new[:, :, WINDOW:]).then_inc(qkt_evac, 1)

                def exps(n, g):
                    after(act, max_done, 2 * n + (g + 1))
                    after(act, probs_n_done, 2 * n + (g - 1))
                    for cw in range(4):
                        k = 4 * g + cw
                        e = act.activation(probs[:, k, :], s_ps[g][:, cw * P:(cw + 1) * P], ACT.Exp,
                                           bias=neg_max[:, k:k + 1], accum_out=row_sum[:, k:k + 1])
                    e.then_inc(probs_done, 1)

                def take_probs(n, parity):
                    after(act, pt_ready, 2 * n + 2)
                    after(act, ot_ready, n - 1)
                    act.copy(probs_t[parity][:, 4:8, :],
                             s_ps[1].rearrange("p (c k) -> p c k", c=4)).then_inc(pt_evac[1], 1)

                def take_o(n):
                    after(act, ot_ready, n + 1)
                    after(act, y_ready, n)
                    act.copy(o_t[:], ot_ps).then_inc(ot_evac, 1)

                def square(j):
                    jj = SPANS * layer + j
                    after(act, cen_ready, jj + 1)
                    after(act, ss_done, 2 * TILES * (layer + 1))
                    after(act, var_ready, jj)
                    act.activation(ln_sq, cen_ps[j % 2], ACT.Square).then_inc(ln_sq_done, 1)

                def norm_rstd(j):
                    jj = SPANS * layer + j
                    after(act, var_ready, jj + 1)
                    act.activation(ln_log, var_ps, ACT.Ln, bias=eps_s[:, 0:1]).then_inc(ln_log_done, 1)
                    after(act, ln_log_done, jj + 1)
                    after(act, rot_done, 3 * TILES * (layer + 1))
                    after(act, hn_scaled, jj - 1)
                    act.activation(ln_rstd[j % 2], ln_log, ACT.Exp, scale=-0.5).then_inc(ln_rstd_done, 1)

                def step(t, parity):
                    n = t + layer * TILES
                    j = norm_span(t)
                    if there(t):
                        exps(n, 0)
                        exps(n, 1)
                    if j is not None:
                        square(j)
                    if there(t + 2) and not is_at(t, -1):
                        norms(n + 2)
                    if there(t + 1):
                        take_q(n + 1)
                        take_k(n + 1, 1 - parity)
                    if there(t + 2):
                        inverse_norms(n + 2)
                    if there(t):
                        take_probs(n, parity)
                    if there(t + 1):
                        pass_k_on(1 - parity, is_at(t, TILES - 2))
                    if there(t - 1):
                        take_o(n - 1)
                    if j is not None:
                        norm_rstd(j)
                    if there(t + 1):
                        take_v(n + 1, 1 - parity)

                over_tiles(act, step)

                act.preload_act_table_set("gelu_and_others")
                if layer == 0:
                    act.wait_ge(fw_in, 16 * 5)

                def span(j):
                    jj = j + SPANS * layer
                    early = early_tile(layer, j)
                    for c, (at, size) in enumerate(HID_PARTS):
                        after(act, gate_ready, 3 * jj + (c + 1))
                        after(act, hh_done, 3 * jj if c < 2 else 3 * jj + 1)
                        act.activation(gelu_s[c % 2][0:size, :], gate_ps[c % 2][0:size, :], ACT.Gelu,
                                       bias=b1_s[0:size, layer, 1, c:c + 1]).then_inc(gelu_done, 1)
                        if is_at(j, 1) and c == 0:
                            square(SPANS - 1)
                    if early is not None:
                        norms(TILES * (layer + 1) + early)
                    if early is not None or is_at(j, 1):
                        act.preload_act_table_set("natural_log_exp_and_others")
                        if is_at(j, 1):
                            norm_rstd(SPANS - 1)
                        elif early == 0:
                            inverse_norms(TILES * (layer + 1) + early)
                        if layer == LAYERS - 1 or j < SPANS - 1:
                            act.preload_act_table_set("gelu_and_others")

                for j in range(SPANS):
                    span(j)
        @block.vector
        def _(dve):
            def input_stats(g):
                dve.wait_ge(x_in[g], 16)
                for t in range(4 * g, 4 * g + 4):
                    dve.bn_stats(stats[:, t, :], x_raw[:, t, :]).then_inc(stat_done, 1)
                for t in range(4 * g, 4 * g + 4):
                    dve.wait_ge(stat_done, t + 1)
                    dve.bn_aggr(mv[:, t, :], stats[:, t, :]).then_inc(mv_done, 1)

            def stage_patches(t):
                after(dve, a_vr_done, t)
                dve.tensor_copy(a_x, xin[:, cols(t * A_STEP + 1, A_WIN)]).then_inc(a_staged, 1)
                after(dve, a_staged, 3 * t + 1)
                for s in range(SHIFT):
                    of = a_x[:, 0:A_STEP].rearrange("p (b i s) -> p b i s", b=2, s=SHIFT)[:, :, :, s]
                    dve.tensor_copy(a_rep.rearrange("p (b s) r i -> p b s r i", s=SHIFT)[:, :, s],
                                    of.unsqueeze(2).broadcast_to([P, 2, 4, PATCH])).then_inc(a_staged, 1)

            def patch_values(t, parity):
                after(dve, a_vr_done, t + 1)
                after(dve, a_op_done, t - 1)
                dve.tensor_tensor(a_v[parity], a_vr[0:4 * PATCH, :].rearrange("p (j d) -> p j d", j=4),
                                  value_mask[0:4 * PATCH, :].unsqueeze(1).broadcast_to([4 * PATCH, 4, DIM]),
                                  ALU.mult).then_inc(a_v_done, 1)

            def patch_differences(t):
                s4 = a_s.rearrange("p g (h k) -> p g h k", h=4)
                after(dve, a_s_done, t + 1)
                dve.tensor_reduce(a_max[:], s4, AX.X, ALU.max).then_inc(a_max_done, 1)
                after(dve, a_max_done, t + 1)
                after(dve, a_p_done, t)
                dve.tensor_tensor(a_dif[:].rearrange("p (g h) k -> p g h k", g=4), s4,
                                  a_max[:].rearrange("p (g h) -> p g h", g=4).unsqueeze(3)
                                  .broadcast_to([P, 4, 4, PATCH]), ALU.subtract).then_inc(a_dif_done, 1)

            def put_patches(t):
                after(dve, a_ot_done, t + 1)
                blocks = PATCH_BLOCKS - 2 * (A_STEPS - 1) if is_at(t, A_STEPS - 1) else 2
                for s in range(SHIFT):
                    to = x_patch[:, cols(t * A_STEP, A_STEP)].rearrange("p (b i s) -> p b i s", b=2, s=SHIFT)
                    of = a_op[:, P:2 * P].rearrange("p (b s i) -> p b s i", b=2, s=SHIFT)
                    o = dve.tensor_copy(to[:, 0:blocks, :, s], of[:, 0:blocks, s, 0:PATCH])
                o.then_inc(a_out_done, 1)

            def patch_step(t, parity):
                if there(t + 1, A_STEPS):
                    stage_patches(t + 1)
                if there(t - 2, A_STEPS):
                    put_patches(t - 2)
                if is_at(t, A_STEPS - 1):
                    split_stage(0, 0)
                    split_stage(1, 1)
                if there(t, A_STEPS):
                    patch_values(t, parity)
                    patch_differences(t)
                    after(dve, a_p_done, t + 1)
                    dve.reduce_sum(a_sum[:], a_p, AX.X).then_inc(a_sum_done, 1)
                    after(dve, a_sum_done, t + 1)
                    dve.reciprocal(a_inv[:], a_sum[:]).then_inc(a_inv_done, 1)
                if there(t - 1, A_STEPS):
                    after(dve, a_op_done, t)
                    dve.tensor_copy(a_o[:], a_op[:, 0:DIM]).then_inc(a_o_done, 1)
                if there(t, A_STEPS):
                    after(dve, a_inv_done, t + 1)
                    after(dve, a_tp_done, t)
                    dve.tensor_tensor(a_pn, a_p, a_inv[:].unsqueeze(2).broadcast_to([P, A_HEADS, PATCH]),
                                      ALU.mult).then_inc(a_pn_done, 1)

            def split_stage(n, parity):
                after(dve, staged_raw, 2 * n + 2)
                after(dve, v_ready, n - 1)
                dve.tensor_copy(stage_hi[parity][:], stage[parity][:]).then_inc(staged_hi, 1)
                after(dve, staged_hi, n + 1)
                dve.tensor_tensor(stage_lo[parity][:], stage[parity][:], stage_hi[parity][:],
                                  ALU.subtract).then_inc(staged, 1)

            def sum_squares(n):
                after(dve, sq_done, n + 1)
                dve.reduce_sum(ss[:], sq[:].rearrange("p (h d) -> p h d", d=DH), AX.X).then_inc(ss_done, 1)
                after(dve, ss_done, 2 * n + 1)
                dve.tensor_scalar(ssc[:], ss[:], NORM_FLOOR_SQ, None, ALU.max).then_inc(ss_done, 1)

            def unit(n):
                after(dve, rnorm_done, n + 1)
                after(dve, rot_done, 3 * n)
                dve.tensor_tensor(qkn[:].rearrange("p (h d) -> p h d", d=DH),
                                  qk_ps.rearrange("p (h d) -> p h d", d=DH),
                                  rnorm[:].unsqueeze(2).broadcast_to([P, 2 * HEADS, DH]),
                                  ALU.mult).then_inc(qkn_done, 1)

            def rotate_cos(n, t):
                cos = cos_w[:, cols(t, 1), :, :].rearrange("p a b d -> p (a b) d")
                dve.tensor_tensor(rot1[:].rearrange("p (a h d) -> p a h d", a=2, d=DH),
                                  qkn[:].rearrange("p (a h d) -> p a h d", a=2, d=DH),
                                  cos.unsqueeze(2).broadcast_to([P, 2, HEADS, DH]),
                                  ALU.mult).then_inc(rot_done, 1)

            def rotate_sin(n, t, half):
                after(dve, qkn_done, n + 1)
                after(dve, qkt_ready, 2 * n)
                of, to = half * HALF, (1 - half) * HALF
                sin = sin_w[:, cols(t, 1), :, of:of + HALF].rearrange("p a b d -> p (a b) d")
                dve.tensor_tensor(rot2[:].rearrange("p (a h d) -> p a h d", a=2, d=DH)[:, :, :, to:to + HALF],
                                  qkn[:].rearrange("p (a h d) -> p a h d", a=2, d=DH)[:, :, :, of:of + HALF],
                                  sin.unsqueeze(2).broadcast_to([P, 2, HEADS, HALF]),
                                  ALU.mult).then_inc(rot_done, 1)

            def sum_rotated(n, part):
                after(dve, rot_done, 3 * n + 3)
                half = slice(part * INNER, (part + 1) * INNER)
                dve.tensor_tensor(rot2[:, half], rot2[:, half], rot1[:, half], ALU.add).then_inc(rot_summed, 1)

            def rotate(n, t):
                rotate_sin(n, t, 0)
                rotate_sin(n, t, 1)
                rotate_cos(n, t)

            def normalize_input(g):
                dve.wait_ge(rstd0_done, g + 1)
                for t in range(4 * g, 4 * g + 4):
                    dve.tensor_scalar(xn_tok[:, t, :], x_raw[:, t, :], mv[:, t, 0:1], rstd0[:, t:t + 1],
                                      ALU.subtract, ALU.mult).then_inc(xn_done, 1)

            def in_front(t):
                if t == -1:
                    input_stats(0)
                    normalize_input(0)
                    input_stats(1)
                    dve.wait_ge(const_in, 16)
                    dve.wait_ge(xin0_done, 1)
                if t == 0:
                    normalize_input(1)
                    input_stats(2)
                    input_stats(3)
                    normalize_input(2)
                    normalize_input(3)
                if t == 1:
                    dve.wait_ge(xin0_done, 2)
                if t == A_STEPS:
                    sum_squares(0)

            over_patches(dve, patch_step, in_front)
            unit(0)
            put_patches(A_STEPS - 1)
            dve.wait_ge(tables_done, 4)
            rotate(0, 0)
            sum_rotated(0, 0)
            sum_rotated(0, 1)
            sum_squares(1)

            for layer in range(LAYERS):
                def maxima(n, g):
                    after(dve, s_ready, 2 * n + (g + 1))
                    dve.tensor_reduce(neg_max[:, 4 * g:4 * g + 4], s_ps[g].rearrange("p (c k) -> p c k", c=4),
                                      AX.X, ALU.max, negate=True).then_inc(max_done, 1)

                def invert(n, g):
                    after(dve, probs_done, 2 * n + (g + 1))
                    dve.reciprocal(row_inv[:, 4 * g:4 * g + 4], row_sum[:, 4 * g:4 * g + 4]).then_inc(inv_done, 1)

                def take_probs(n, parity):
                    after(dve, pt_ready, 2 * n + 1)
                    after(dve, ot_ready, n - 1)
                    dve.tensor_copy(probs_t[parity][:, 0:4, :],
                                    s_ps[0].rearrange("p (c k) -> p c k", c=4)).then_inc(pt_evac[0], 1)

                def residual(n, t):
                    after(dve, y_ready, n + 1)
                    dve.tensor_tensor(x1[:, cols(t * P, P)], y_ps[:, 0:P], xin[:, cols(t * P + 1, P)],
                                      ALU.add).then_inc(x1_done, 1)

                def normalize(j):
                    jj = SPANS * layer + j
                    span = slice(j * WIDE, (j + 1) * WIDE)
                    after(dve, ln_rstd_done, jj + 1)
                    dve.tensor_tensor(hn[:, span], cen_ps[j % 2], ln_rstd[j % 2], ALU.mult).then_inc(hn_scaled, 1)
                    after(dve, hn_scaled, jj + 1)
                    dve.tensor_scalar(hn[:, span], hn[:, span], vec_s[:, layer:layer + 1],
                                      vec_s[:, 2 + layer:3 + layer], ALU.mult, ALU.add).then_inc(hn_done, 1)

                def split_normalized(j):
                    jj = SPANS * layer + j
                    span = slice(j * WIDE, (j + 1) * WIDE)
                    after(dve, hn_done, jj + 1)
                    dve.tensor_copy(hn_hi[:, span], hn[:, span]).then_inc(hn_split, 1)
                    after(dve, hn_split, 2 * jj + 1)
                    dve.tensor_tensor(hn_lo[:, span], hn[:, span], hn_hi[:, span], ALU.subtract).then_inc(hn_split, 1)

                def step(t, parity):
                    n = t + layer * TILES
                    turned = there(t + 1) and not is_at(t, -1)
                    if there(t):
                        maxima(n, 0)
                    if there(t + 2) and not is_at(t, -1):
                        split_stage(n + 2, parity)
                    if there(t):
                        maxima(n, 1)
                    if turned:
                        rotate_sin(n + 1, t + 1, 0)
                    if there(t - 2):
                        residual(n - 2, t - 2)
                    if there(t):
                        invert(n, 0)
                    if turned:
                        rotate_sin(n + 1, t + 1, 1)
                        sum_rotated(n + 1, 0)
                    if there(t):
                        invert(n, 1)
                    if turned:
                        sum_rotated(n + 1, 1)
                    if there(t + 2) and not is_at(t, -1):
                        sum_squares(n + 2)
                    if there(t):
                        take_probs(n, parity)
                    if there(t + 2):
                        unit(n + 2)
                    if norm_span(t - 1) is not None:
                        normalize(norm_span(t - 1))
                        split_normalized(norm_span(t - 1))

                if layer == 0:
                    dve.wait_ge(fw_in, 16 * 5)
                over_tiles(dve, step)

                if layer == LAYERS - 1:
                    dve.tensor_tensor(b2_out[:], vec_s[:, 5:6], vec_s[:, 6:7], ALU.add).then_inc(b2_done, 1)
                    dve.wait_ge(b2_done, 1)

                def put_out(j):
                    after(dve, tr_ready, j + 1)
                    after(dve, stored, 16 * j)
                    dve.tensor_tensor(out_s[:], tr_ps,
                                      x_raw[:].rearrange("p t d -> p (t d)")[:, cols(j * WIDE, WIDE)],
                                      ALU.add).then_inc(out_done, 1)

                def span(j):
                    jj = j + SPANS * layer
                    early = early_tile(layer, j)
                    for c, (at, size) in enumerate(HID_PARTS):
                        after(dve, gelu_done, 3 * jj + (c + 1))
                        after(dve, lin_ready, 3 * jj + (c + 1))
                        after(dve, ffn_ready, jj)
                        dve.scalar_tensor_tensor(hh[c][0:size, :], lin_ps[c % 2][0:size, :],
                                                 b1_s[0:size, layer, 0, c:c + 1], gelu_s[c % 2][0:size, :],
                                                 ALU.add, ALU.mult).then_inc(hh_done, 1)
                        if early == 0 and c < 2:
                            split_stage(TILES * (layer + 1) + c, c)
                        if is_at(j, 2) and c == 1:
                            split_normalized(SPANS - 1)
                        if early == 1 and c == 1:
                            dve.wait_ge(tables_done, 4 * (layer + 2))
                            rotate(TILES * (layer + 1), 0)
                    if early == 1:
                        sum_rotated(TILES * (layer + 1), 0)
                        sum_rotated(TILES * (layer + 1), 1)
                    if early is not None:
                        sum_squares(TILES * (layer + 1) + early)
                    if layer == LAYERS - 1 and there(j - 1, SPANS):
                        put_out(j - 1)
                    after(dve, ffn_ready, jj + 1)
                    if layer < LAYERS - 1:
                        dve.scalar_tensor_tensor(xin[:, cols(j * WIDE + 1, WIDE)], ffn_ps,
                                                 vec_s[:, 4 + layer:5 + layer], x1[:, cols(j * WIDE, WIDE)],
                                                 ALU.add, ALU.add).then_inc(x2_done, 1)
                        if early == 0:
                            unit(TILES * (layer + 1))
                    else:
                        dve.scalar_tensor_tensor(sum_t, ffn_ps, b2_out[:], x1[:, cols(j * WIDE, WIDE)],
                                                 ALU.add, ALU.add).then_inc(x2_done, 1)
                    if is_at(j, 1):
                        normalize(SPANS - 1)

                for j in range(SPANS):
                    span(j)
                if layer == LAYERS - 1:
                    put_out(SPANS - 1)


def kernel(**inputs):
    import concourse.bacc as bacc
    from concourse.bass_utils import run_bass_kernel_spmd

    named = {
        "x": inputs["L0_attn_x"],
        "a_wqkv_t": np.transpose(inputs["L0_attn_Wqkv"]),
        "a_wout_t": np.transpose(inputs["L0_attn_Wout"]),
        "wqkv": inputs["L0_ffn_wqkv"],
        "q_scale": inputs["L0_ffn_q_scale"],
        "k_scale": inputs["L0_ffn_k_scale"],
        "wo": inputs["L0_ffn_wo"],
        "w1": inputs["L0_ffn_w1"],
        "w2": inputs["L0_ffn_w2"],
        "vectors": pack_vectors(**{k: inputs["L0_" + k] for k in
                                   ("ffn_b1", "ffn_ln_g", "ffn_ln_b", "ffn_b2", "attn_bout")}),
        **constants(),
    }
    nc = bacc.Bacc("TRN2", target_bir_lowering=False, num_devices=1)
    arrays, args = {}, []
    for name, a in named.items():
        a = np.ascontiguousarray(a)
        arrays[f"in_{name}"] = a
        args.append(nc.dram_tensor(f"in_{name}", a.shape, mybir.dt.from_np(a.dtype), kind="ExternalInput").ap())
    out = nc.dram_tensor("out", (1, N, DIM), F32, kind="ExternalOutput").ap()
    build(nc, *args, out)
    r = run_bass_kernel_spmd(nc, [arrays], core_ids=[0])
    return r.results[0]["out"]
```
